# Optimizing a Trainium2 kernel written in Bass

```python
import numpy as np
import jax
import jax.numpy as jnp

def _softmax(x, axis=-1):
    return jax.nn.softmax(x, axis=axis)

def _gelu(x):
    return jax.nn.gelu(x, approximate=True)

def _silu(x):
    return jax.nn.silu(x)

def _sigmoid(x):
    return jax.nn.sigmoid(x)

def _layernorm(x, axis=-1, eps=1e-05):
    m = jnp.mean(x, axis=axis, keepdims=True)
    v = jnp.var(x, axis=axis, keepdims=True)
    return (x - m) / jnp.sqrt(v + eps)

def _scatter_add(tgt, idx, src, axis=0):
    return tgt.at[idx].add(src)

def _segment_sum(src, seg, n):
    return jax.ops.segment_sum(src, seg, n)
kernel_name = 'mk_metaformer_d1_conv_nchw2048_r4_ada68d'

def setup_inputs(seed: int=0):
    np.random.seed(seed)
    _w = jnp.asarray

    def _rec_inputs():
        import jax
        import jax.numpy as jnp
        _gk = jax.random.key(seed)
        x = -7.109e-05 + 0.9999 * jax.random.normal(jax.random.fold_in(_gk, 1), (8, 512, 16, 16), jnp.float32)
        return x
    x = _rec_inputs()

    def _L0_conv_setup():
        import jax, jax.numpy as jnp
        import numpy as np
        BN_EPS = 1e-05
        key = jax.random.key(seed)
        k1, k2 = jax.random.split(key)
        B, C, H, W = (8, 512, 16, 16)
        x = jax.random.normal(k1, (B, C, H, W), dtype=jnp.float32)
        cfc_w = jax.random.normal(k2, (C, 3), dtype=jnp.float32) * 0.1
        bn_w = jnp.ones((C,), dtype=jnp.float32)
        bn_b = jnp.zeros((C,), dtype=jnp.float32)
        return {'x': x, 'cfc_w': cfc_w, 'bn_w': bn_w, 'bn_b': bn_b}
    _L0_conv_all = _L0_conv_setup()
    _L0_conv_in = {k: v for k, v in _L0_conv_all.items() if k in ('cfc_w', 'bn_w', 'bn_b')}
    del _L0_conv_all

    def _L0_ffn_setup():
        import jax, jax.numpy as jnp
        import numpy as np

        def _glu(x, wg, wu, wd):
            return jax.nn.silu(x @ wg) * (x @ wu) @ wd
        key = jax.random.key(seed)
        ks = jax.random.split(key, 8)
        B, S, H, I, E = (4, 512, 512, 512, 8)
        s = 0.02
        return {'hidden_states': jax.random.normal(ks[0], (B, S, H), jnp.float32), 'router_w': jax.random.normal(ks[1], (E, H), jnp.float32) * s, 'w1': jax.random.normal(ks[2], (E, H, I), jnp.float32) * s, 'v1': jax.random.normal(ks[3], (E, H, I), jnp.float32) * s, 'w2': jax.random.normal(ks[4], (E, I, H), jnp.float32) * s, 'shared_gate': jax.random.normal(ks[5], (I, H), jnp.float32) * s, 'shared_up': jax.random.normal(ks[6], (I, H), jnp.float32) * s, 'shared_down': jax.random.normal(ks[7], (H, I), jnp.float32) * s}
    _L0_ffn_all = _L0_ffn_setup()
    _L0_ffn_in = {k: v for k, v in _L0_ffn_all.items() if k in ('router_w', 'w1', 'v1', 'w2', 'shared_gate', 'shared_up', 'shared_down')}
    del _L0_ffn_all
    return {'x': x, 'L0_conv_cfc_w': _L0_conv_in['cfc_w'], 'L0_conv_bn_w': _L0_conv_in['bn_w'], 'L0_conv_bn_b': _L0_conv_in['bn_b'], 'L0_ffn_router_w': _L0_ffn_in['router_w'], 'L0_ffn_w1': _L0_ffn_in['w1'], 'L0_ffn_v1': _L0_ffn_in['v1'], 'L0_ffn_w2': _L0_ffn_in['w2'], 'L0_ffn_shared_gate': _L0_ffn_in['shared_gate'], 'L0_ffn_shared_up': _L0_ffn_in['shared_up'], 'L0_ffn_shared_down': _L0_ffn_in['shared_down']}

def reference(x, L0_conv_cfc_w, L0_conv_bn_w, L0_conv_bn_b, L0_ffn_router_w, L0_ffn_w1, L0_ffn_v1, L0_ffn_w2, L0_ffn_shared_gate, L0_ffn_shared_up, L0_ffn_shared_down):
    import jax
    import jax.numpy as jnp

    def _L0_conv_ref(x, cfc_w, bn_w, bn_b):
        import jax, jax.numpy as jnp
        import numpy as np
        BN_EPS = 1e-05
        b, c, h, w = x.shape
        xf = x.reshape(b, c, h * w)
        mean = jnp.mean(xf, axis=-1)
        mx = jnp.max(xf, axis=-1)
        std = jnp.std(xf, axis=-1, ddof=1)
        u = jnp.stack([mean, mx, std], axis=-1)
        med = jnp.median(u.reshape(b, -1), axis=-1)[:, None, None]
        u = jax.lax.stop_gradient((u - med) ** 3)
        z = jnp.einsum('bck,ck->bc', u, cfc_w)
        z = z / jnp.sqrt(jnp.float32(1.0) + BN_EPS) * bn_w + bn_b
        g = jax.nn.sigmoid(z)
        return x * g[:, :, None, None]

    def _L0_ffn_ref(hidden_states, router_w, w1, v1, w2, shared_gate, shared_up, shared_down):
        import jax, jax.numpy as jnp
        import numpy as np

        def _glu(x, wg, wu, wd):
            return jax.nn.silu(x @ wg) * (x @ wu) @ wd
        B, S, H = hidden_states.shape
        E = router_w.shape[0]
        TOP_K = 1
        x = hidden_states.reshape(-1, H)
        T = x.shape[0]
        logits = x @ router_w.T
        top_vals, top_idx = jax.lax.top_k(logits, TOP_K)
        expert_weights = jax.nn.sigmoid(top_vals)
        dense_w = jnp.zeros((T, E), x.dtype).at[jnp.arange(T)[:, None], top_idx].set(expert_weights)
        out = jnp.zeros_like(x)
        for e in range(E):
            y = _glu(x, w1[e], v1[e], w2[e])
            out = out + dense_w[:, e:e + 1] * y
        out = out + _glu(x, shared_gate.T, shared_up.T, shared_down.T)
        return out.reshape(B, S, H)

    def _gn(v, G=32, eps=1e-05):
        B_, C_, H_, W_ = v.shape
        g = v.reshape(B_, G, C_ // G, H_, W_)
        m = jnp.mean(g, axis=(2, 3, 4), keepdims=True)
        s = jnp.var(g, axis=(2, 3, 4), keepdims=True)
        return ((g - m) / jnp.sqrt(s + eps)).reshape(v.shape)

    def _ln_c(v, eps=1e-06):
        m = jnp.mean(v, axis=1, keepdims=True)
        s = jnp.var(v, axis=1, keepdims=True)
        return (v - m) / jnp.sqrt(s + eps)

    def _ln_t(v, eps=1e-05):
        m = jnp.mean(v, axis=-1, keepdims=True)
        s = jnp.var(v, axis=-1, keepdims=True)
        return (v - m) / jnp.sqrt(s + eps)

    def _to_tokens(v):
        B_, C_, H_, W_ = v.shape
        return v.reshape(B_, C_, H_ * W_).transpose(0, 2, 1)

    def _from_tokens(t, like):
        B_, C_, H_, W_ = like.shape
        return t.transpose(0, 2, 1).reshape(B_, C_, H_, W_)
    x = x + _L0_conv_ref(_ln_c(x), L0_conv_cfc_w, L0_conv_bn_w, L0_conv_bn_b)
    t = _to_tokens(x)
    t = t + _L0_ffn_ref(_ln_t(t), L0_ffn_router_w, L0_ffn_w1, L0_ffn_v1, L0_ffn_w2, L0_ffn_shared_gate, L0_ffn_shared_up, L0_ffn_shared_down)
    x = _from_tokens(t, x)
    return x

_drawn_inputs = setup_inputs


def setup_inputs(seed=0):
    import zlib

    import numpy as np

    out = dict(_drawn_inputs(seed))
    spreads = {'L0_conv_bn_w': (1.0, 0.6), 'L0_conv_bn_b': (0.0, 0.522)}
    factors = {'L0_ffn_router_w': 2.829, 'L0_ffn_w1': 2.685}
    for name, (base, spread) in spreads.items():
        noise = np.random.default_rng([zlib.crc32(name.encode()), seed]).standard_normal(out[name].shape)
        drawn = base * np.exp(spread * noise) if base else spread * noise
        out[name] = jnp.asarray(drawn.astype(out[name].dtype))
    for name, factor in factors.items():
        out[name] = (out[name] * factor).astype(out[name].dtype)
    return out
```

```python
from contextlib import ExitStack

import concourse.bass as bass
from concourse import mybir

F32 = mybir.dt.float32
F32R = mybir.dt.float32r
BF16 = mybir.dt.bfloat16
I32 = mybir.dt.int32
U32 = mybir.dt.uint32
ALU = mybir.AluOpType
ACT = mybir.ActivationFunctionType
AX_X = mybir.AxisListType.X
ds = bass.ds

P = 128
LN_C_EPS = 1e-6
LN_T_EPS = 1e-5
BN_EPS = 1e-5
BIG = 1e30
MEAN, STD, MAX = range(3)
GATE, UP, DOWN = range(3)
HI, LO = range(2)
RING = 4
SEARCH_FROM, SEARCH_TO = -24.0, 24.0
SEARCH_STEPS = 7
N_CONSTS = 12
SLOT_COL, OTHER_COL, READY_COL, FIRST_COL, LOADED_COL, FLAG_COL, COLS = 0, 1, 2, 3, 4, 5, 8


def program(nc, x_tok, conv_par, router, weights, xn_d, z_d, out):
    T, C = x_tok.shape
    B = 8
    TPB = T // B
    NT = T // P
    KC = C // P
    E = router.shape[1] // KC
    NSETS = weights.shape[0]
    NB = NT + E - 1
    NV = 3 * C
    TPART = P // B
    N_ROUTED = NT
    assert C == 512 and KC == 4 and TPB == 2 * P and NSETS == E + 1 and E == 8

    with ExitStack() as ctx:
        def sb(name, shape, dt=F32):
            return ctx.enter_context(nc.sbuf_tensor(name, shape, dt))

        def ps(name, shape, dt=F32):
            return ctx.enter_context(nc.psum_tensor(name, shape, dt))

        def sem(name):
            return ctx.enter_context(nc.semaphore(name))

        x_sb = sb("x_sb", [P, NT, C])
        wbuf = sb("wbuf", [P, 2, 3, 2, KC, C], F32R)
        wraw = sb("wraw", [P, 3, KC, C])
        xT = sb("xT", [P, RING, 2, KC, P], F32R)
        aring = sb("aring", [P, RING, C])
        sg = sb("sg", [P, 2, C])
        hT = sb("hT", [P, 2, 2, KC, P], F32R)
        xg = sb("xg", [P, 2, C])
        scratch = sb("scratch", [P, 2176])
        diag = xg
        zg = x_sb[:, 0:2, :]
        ident = sb("ident", [P, P])
        ones = sb("ones", [P, P])
        bdiag = sb("bdiag", [P, B, TPART])
        upper = sb("upper", [P, P], BF16)
        ones_bf = sb("ones_bf", [P, P], BF16)
        iota_f = sb("iota_f", [P, P])
        iota_i = scratch[:, 0:P].bitcast(I32)
        sel8 = sb("sel8", [P, B])
        pidx_i = sb("pidx_i", [P, 2], I32)
        pidx = sb("pidx", [P, 2])
        i128 = sb("i128", [P, NT])
        rev8 = sb("rev8", [P, E])
        par = sb("par", [P, KC * 5])
        rt = sb("rt", [P, KC, E])
        rhl = sb("rhl", [P, KC, 2, E], F32R)
        bnst = sb("bnst", [P, 4, 6])
        mva = sb("mva", [P, NT, 2])
        rsa = sb("rsa", [P, NT])
        mvb = sb("mvb", [P, RING, 2])
        rsb = sb("rsb", [P, RING])
        cpow = sb("cpow", [P, 4, B * KC])
        U = sb("U", [P, B, KC, 3])
        U2 = aring[:, 3, 0:B * KC * 3].rearrange("p (b s) -> p b s", b=B)
        steps = sb("steps", [P, 2, SEARCH_STEPS])
        med = sb("med", [P, 16])
        medd = sb("medd", [P, B])
        zt = sb("zt", [P, B, KC])
        g = sb("g", [P, B + 1, KC])
        lraw = sb("lraw", [P, NT, 2 * E])
        w_rt = sb("w_rt", [P, NT])
        tab = sb("tab", [1, NB + 1, COLS], I32)
        slotinfo = sb("slotinfo", [P, 3, NB])
        tokidx = sb("tokidx", [P, NB], U32)
        scatidx = sb("scatidx", [P, NB], U32)
        eps_t = sb("eps_t", [P, 1])

        rtmp = xg[:, :, :].rearrange("p a c -> p (a c)")

        GU = ps("GU", [P, 4, C])
        th = ps("th", [P, C])
        tx = ps("tx", [P, C])
        yb = ps("yb", [P, C])
        ms = ps("ms", [P, C])

        x_in = [sem(f"x_in{b}") for b in range(B)]
        par_in = sem("par_in")
        rt_in = sem("rt_in")
        w_in = [sem(f"w_in{k}") for k in range(3)]
        whi = sem("whi")
        wlo = sem("wlo")
        t_norm = sem("t_norm")
        t_gated = sem("t_gated")
        t_x1 = sem("t_x1")
        t_bn = sem("t_bn")
        t_eps = sem("t_eps")
        s_cnt = sem("s_cnt")
        s_low = sem("s_low")
        s_thr = sem("s_thr")
        iotas = sem("iotas")
        consts = sem("consts")
        dv = sem("dv")
        pl = sem("pl")
        stats_a = sem("stats_a")
        rstd_a = sem("rstd_a")
        a_ready = sem("a_ready")
        aT_ready = sem("aT_ready")
        chan_done = sem("chan_done")
        std_done = sem("std_done")
        ub_ready = sem("ub_ready")
        v_ready = sem("v_ready")
        below = sem("below")
        n_below = sem("n_below")
        medd_ready = sem("medd_ready")
        med_b = sem("med_b")
        z_ready = sem("z_ready")
        g_ready = sem("g_ready")
        diag_ready = sem("diag_ready")
        gate_bc = sem("gate_bc")
        gate_used = sem("gate_used")
        stats_b = sem("stats_b")
        rstd_b = sem("rstd_b")
        xn_ready = sem("xn_ready")
        xn_out = [sem(f"xn_out{u}") for u in range(RING)]
        tx_done = sem("tx_done")
        xhi = sem("xhi")
        xlo = sem("xlo")
        rhl_ready = sem("rhl_ready")
        logits = sem("logits")
        logits_used = sem("logits_used")
        g_done = sem("g_done")
        u_done = sem("u_done")
        silu = sem("silu")
        hid = sem("hid")
        th_done = sem("th_done")
        hhi = sem("hhi")
        hlo = sem("hlo")
        y_done = sem("y_done")
        y_used = sem("y_used")
        z_out = sem("z_out")
        onehot_ready = sem("onehot_ready")
        w_ready = sem("w_ready")
        rank_done = sem("rank_done")
        sel_ready = sem("sel_ready")
        slots_done = sem("slots_done")
        tables = sem("tables")
        slots_ready = sem("slots_ready")
        x1_kept = sem("x1_kept")
        xg_in = [sem(f"xg_in{u}") for u in range(2)]
        zg_in = [sem(f"zg_in{u}") for u in range(2)]
        o_out = [sem(f"o_out{u}") for u in range(2)]

        block = ctx.enter_context(nc.Block())

        def gu(parity, which):
            return GU[:, 2 * parity + which, :]

        def wset(q, k, part, kc):
            if isinstance(q, int):
                return wbuf[:, q, k, part, kc, :]
            return wbuf[:, ds(q, 1), k, part, kc, :].rearrange("p a c -> p (a c)")

        def tile_of(buf, t):
            if isinstance(t, int):
                return buf[:, t, :]
            return buf[:, ds(t, 1), :].rearrange("p a c -> p (a c)")

        def table_row(eng, c):
            bounds = {READY_COL: 3 * NSETS, FIRST_COL: NB, LOADED_COL: 16 * (NSETS + 1)}
            return [eng.value_load(tab[0:1, ds(c, 1), col], min_val=0, max_val=bounds.get(col, 1)) for col in range(COLS)]

        @block.sync
        def _(sp):
            def load_w(q, k):
                src = weights[q, k] if isinstance(q, int) else weights[ds(q, 1), k, :, :].rearrange("a p n -> (a p) n")
                sp.dma_start(wraw[:, k, :, :].rearrange("p k c -> p (k c)"), src).then_inc(w_in[k], 16)

            xv = x_tok.rearrange("(b t p) c -> b p t c", p=P, t=2)
            for b in range(B):
                sp.dma_start(x_sb[:, 2 * b:2 * b + 2, :], xv[b]).then_inc(x_in[b], 16)
            sp.dma_start(par[:, :], conv_par).then_inc(par_in, 16)
            sp.dma_start(rt[:, :, :], router.rearrange("p (k e) -> p k e", k=KC)).then_inc(rt_in, 16)
            for k in range(3):
                load_w(0, k)
            for k in range(3):
                sp.wait_ge(wlo, k + 1)
                load_w(1, k)

            def store_xn(t, u):
                sp.wait_ge(xn_ready, t + 1)
                sp.dma_start(xn_d[ds(t * P, P), :], aring[:, u, :]).then_inc(xn_out[u], 16)

            def store_z(t):
                sp.wait_ge(y_used, t + 1)
                sp.dma_start(z_d[ds(t * P, P), :], tile_of(x_sb, t)).then_inc(z_out, 16)

            for t in range(RING):
                store_xn(t, t)
            with sp.Fori(0, NT // RING - 1) as j:
                for u in range(RING):
                    store_xn(j * RING + (RING + u), u)
                    store_z(j * RING + u)
            for k in range(3):
                sp.wait_ge(wlo, 3 + k + 1)
                load_w(2, k)
            for t in range(NT - RING, NT):
                store_z(t)
            with sp.Fori(3, NSETS) as q:
                for k in range(3):
                    sp.wait_ge(wlo, q * 3 + (k - 2))
                    load_w(q, k)

        @block.gpsimd
        def _(pool):
            n_own = [0]

            def own(ins):
                n_own[0] += 1
                ins.then_inc(pl, 1)
                pool.wait_ge(pl, n_own[0])

            bk = lambda row: cpow[:, row, :].rearrange("p (b k) -> p b k", b=B)

            pool.iota(iota_i[:, :], pattern=[[1, P]], base=0, channel_multiplier=0).then_inc(iotas, 1)
            pool.iota(pidx_i[:, :], pattern=[[0, 2]], base=0, channel_multiplier=1).then_inc(iotas, 1)
            pool.memset(cpow[:, 0, :], -0.5).then_inc(consts, 1)
            pool.memset(cpow[:, 1, :], 0.5).then_inc(consts, 1)
            pool.memset(cpow[:, 2, :], -1.0).then_inc(consts, 1)
            pool.memset(cpow[:, 3, :], 2.718281828459045).then_inc(consts, 1)
            pool.memset(eps_t[:, :], LN_T_EPS).then_inc(consts, 1)
            pool.memset(ones[:, :], 1.0).then_inc(consts, 1)
            pool.memset(ones_bf[:, :], 1.0).then_inc(consts, 1)
            pool.memset(g[:, B, :], 0.0).then_inc(consts, 1)
            pool.memset(ident[:, :], 0.0).then_inc(pl, 1)
            pool.memset(sel8[:, :], 0.0).then_inc(pl, 1)
            pool.memset(bdiag[:, :, :], 1.0).then_inc(pl, 1)
            n_own[0] = 3
            own(pool.memset(upper[:, :], 1.0))
            pool.affine_select(out=ident[:, :], in_=ident[:, :], compare_op=ALU.not_equal, fill=1.0, base=0,
                               pattern=[[-1, P]], channel_multiplier=1).then_inc(consts, 1)
            pool.affine_select(out=sel8[:, :], in_=sel8[:, :], compare_op=ALU.not_equal, fill=1.0, base=0,
                               pattern=[[-TPART, B]], channel_multiplier=1).then_inc(consts, 1)
            pool.affine_select(out=upper[:, :], in_=upper[:, :], compare_op=ALU.is_gt, fill=0.0, base=0,
                               pattern=[[1, P]], channel_multiplier=-1).then_inc(consts, 1)
            own(pool.affine_select(out=bdiag[:, :, :], in_=bdiag[:, :, :], compare_op=ALU.is_ge, fill=0.0, base=0,
                                   pattern=[[-TPART, B], [0, TPART]], channel_multiplier=1))
            pool.affine_select(out=bdiag[:, :, :], in_=bdiag[:, :, :], compare_op=ALU.is_ge, fill=0.0,
                               base=TPART - 1, pattern=[[TPART, B], [0, TPART]], channel_multiplier=-1).then_inc(consts, 1)
            pool.wait_ge(consts, N_CONSTS)

            for b in range(B):
                pool.wait_ge(stats_a, b + 1)
                own(pool.tensor_scalar(rsa[:, 2 * b:2 * b + 2], mva[:, 2 * b:2 * b + 2, 1], LN_C_EPS, None, ALU.add))
                pool.tensor_tensor(rsa[:, 2 * b:2 * b + 2], rsa[:, 2 * b:2 * b + 2], cpow[:, 0, 0:2],
                                   ALU.pow).then_inc(rstd_a, 1)
            pool.wait_ge(chan_done, B)
            own(pool.tensor_scalar(zt[:, :, :], U[:, :, :, STD], float(TPB) / (TPB - 1), None, ALU.mult))
            pool.tensor_tensor(U[:, :, :, STD], zt[:, :, :], bk(1), ALU.pow).then_inc(std_done, 1)

            def split_lo(q, k, raw, hi, lo):
                pool.wait_ge(whi, 3 * q + k + 1)
                pool.tensor_tensor(lo, raw, hi.bitcast(F32), ALU.subtract).then_inc(wlo, 1)

            for k in range(3):
                split_lo(0, k, wraw[:, k, :, :], wbuf[:, 0, k, HI, :, :], wbuf[:, 0, k, LO, :, :])

            pool.wait_ge(z_ready, 1)
            own(pool.tensor_tensor(g[:, 0:B, :], bk(3), zt[:, :, :], ALU.pow))
            own(pool.tensor_scalar(g[:, 0:B, :], g[:, 0:B, :], 1.0, None, ALU.add))
            own(pool.tensor_tensor(g[:, 0:B, :], g[:, 0:B, :], bk(2), ALU.pow))

            def spread_diag(b, u):
                src = g[:, b, :] if isinstance(b, int) else g[:, ds(b, 1), :].rearrange("p a k -> p (a k)")
                pool.tensor_tensor(diag[:, u, :].rearrange("p (k c) -> p k c", k=KC),
                                   ident[:, :].unsqueeze(1).to_broadcast([P, KC, P]),
                                   src.unsqueeze(2).to_broadcast([P, KC, P]), ALU.mult).then_inc(diag_ready, 1)

            def rstd_tile(t, u):
                pool.wait_ge(stats_b, t + 1)
                r = rsb[:, u:u + 1]
                pool.tensor_tensor(r, mvb[:, u, 1:2], eps_t[:, 0:1], ALU.add).then_inc(t_eps, 1)
                pool.wait_ge(t_eps, t + 1)
                pool.tensor_tensor(r, r, cpow[:, 0, 0:1], ALU.pow).then_inc(rstd_b, 1)

            spread_diag(0, 0)
            spread_diag(1, 1)
            rstd_tile(0, 0)
            rstd_tile(1, 1)
            spread_diag(2, 0)
            rstd_tile(2, 2)
            rstd_tile(3, 3)
            with pool.Fori(0, NT // RING - 1) as j:
                for u in range(RING):
                    rstd_tile(j * RING + (RING + u), u)
                    if u % 2 == 1:
                        spread_diag(j * 2 + (3 + u // 2), (3 + u // 2) % 2)

            def split_set_1(k):
                split_lo(1, k, wraw[:, k, :, :], wbuf[:, 1, k, HI, :, :], wbuf[:, 1, k, LO, :, :])

            split_set_1(GATE)
            pool.wait_ge(w_ready, 1)
            own(pool.tensor_tensor(w_rt[:, :], cpow[:, 3, 0:NT], w_rt[:, :], ALU.pow))
            own(pool.tensor_scalar(w_rt[:, :], w_rt[:, :], 1.0, None, ALU.add))
            pool.tensor_tensor(w_rt[:, :], w_rt[:, :], cpow[:, 2, 0:NT], ALU.pow).then_inc(w_ready, 1)
            split_set_1(UP)

            def rows(table, b):
                return bass.IndirectOffsetOnAxis(ap=table[:, b:b + 1], axis=0)

            def gather_x(b):
                if b >= 2:
                    pool.wait_ge(tx_done, NT + b - 1)
                pool.indirect_dma_start(xg[:, b % 2, :], None, xn_d[:, :], rows(tokidx, b)).then_inc(xg_in[b % 2], 16)

            def gather_z(b):
                if b >= 2:
                    pool.wait_ge(o_out[b % 2], 16 * (b // 2))
                pool.indirect_dma_start(zg[:, b % 2, :], None, z_d[:, :], rows(tokidx, b)).then_inc(zg_in[b % 2], 16)

            def scatter(b):
                pool.wait_ge(y_used, NT + b + 1)
                pool.indirect_dma_start(out[:, :], rows(scatidx, b), zg[:, b % 2, :], None,
                                        bounds_check=T - 1, oob_is_err=False).then_inc(o_out[b % 2], 16)

            pool.wait_ge(slots_ready, 3)
            for u in range(RING):
                pool.wait_ge(xn_out[u], 16 * (NT // RING))
            gather_x(0)
            gather_x(1)
            split_set_1(DOWN)
            pool.wait_ge(z_out, 16 * NT)
            gather_z(0)
            gather_z(1)
            for b in range(NB):
                if b + 2 < NB:
                    gather_x(b + 2)
                scatter(b)
                if b + 2 < NB:
                    gather_z(b + 2)
            for u in range(2):
                pool.wait_ge(o_out[u], 16 * ((NB + 1 - u) // 2))

        @block.scalar
        def _(act):
            def split_hi(raw, hi):
                act.activation(hi, raw, ACT.Copy).then_inc(whi, 1)

            for q in range(2):
                for k in range(3):
                    act.wait_ge(w_in[k], 16 * (q + 1))
                    split_hi(wraw[:, k, :, :], wbuf[:, q, k, HI, :, :])

            def x_hi(n, slot):
                act.wait_ge(tx_done, n + 1)
                act.activation(xT[:, slot, HI, :, :], tx[:, :].rearrange("p (k t) -> p k t", k=KC), ACT.Copy).then_inc(xhi, 1)

            def silu_gate(n, parity):
                act.wait_ge(g_done, n + 1)
                act.activation(sg[:, parity, :], gu(parity, GATE), ACT.Silu).then_inc(silu, 1)

            def h_hi(n, parity):
                act.wait_ge(th_done, n + 1)
                act.activation(hT[:, parity, HI, :, :], th[:, :].rearrange("p (k t) -> p k t", k=KC), ACT.Copy).then_inc(hhi, 1)

            def keep_x1(t, u):
                act.wait_ge(t_x1, t + 1)
                act.activation(tile_of(x_sb, t), aring[:, u, :], ACT.Copy).then_inc(x1_kept, 1)

            for t in range(RING):
                keep_x1(t, t)
                x_hi(t, t)
            silu_gate(0, 0)
            with act.Fori(0, NT // RING - 1) as j:
                for u in range(RING):
                    n = j * RING + u
                    keep_x1(n + RING, u)
                    h_hi(n, u % 2)
                    silu_gate(n + 1, (u + 1) % 2)
                    x_hi(n + RING, u)
            for n in range(NT - RING, NT):
                h_hi(n, n % 2)
                silu_gate(n + 1, (n + 1) % 2)
                if n >= NT - 2:
                    x_hi(n + 2, n % 2)

            def next_set(c):
                row = table_row(act, c)
                for k in range(3):
                    with act.If(row[FLAG_COL + k] > 0):
                        act.wait_ge(w_in[k], row[LOADED_COL])
                        act.wait_ge(y_done if k == DOWN else u_done, row[FIRST_COL] + NT)
                        split_hi(wraw[:, k, :, :], wbuf[:, ds(row[OTHER_COL], 1), k, HI, :, :].rearrange("p a k c -> p (a k) c"))

            act.wait_ge(tables, 1)
            next_set(0)
            with act.Fori(0, (NB - 3) // 2) as j:
                for u in range(2):
                    n = j * 2 + (NT + u)
                    h_hi(n, u)
                    silu_gate(n + 1, 1 - u)
                    x_hi(n + 2, u)
                    next_set(j * 2 + (u + 1))
            for b in range(NB - 3, NB):
                n = NT + b
                h_hi(n, b % 2)
                if b + 1 < NB:
                    silu_gate(n + 1, (b + 1) % 2)
                if b + 2 < NB:
                    x_hi(n + 2, b % 2)
                    next_set(b + 1)

        @block.vector
        def _(dve):
            n_own = [0]

            def own(ins):
                n_own[0] += 1
                ins.then_inc(dv, 1)
                dve.wait_ge(dv, n_own[0])

            dve.wait_ge(iotas, 2)
            dve.tensor_scalar(pidx_i[:, 1:2], pidx_i[:, 1:2], TPART - 1, None, ALU.bitwise_and).then_inc(dv, 1)
            n_own[0] += 1
            own(dve.tensor_copy(iota_f[:, :], iota_i[:, :]))
            own(dve.tensor_copy(pidx[:, :], pidx_i[:, :]))
            dve.tensor_scalar(i128[:, :], iota_f[:, 0:NT], float(P), None, ALU.mult).then_inc(dv, 1)
            dve.tensor_scalar(rev8[:, :], iota_f[:, 0:E], -1.0, float(E), ALU.mult, ALU.add).then_inc(dv, 1)
            n_own[0] += 2
            width = SEARCH_TO - SEARCH_FROM
            for i in range(SEARCH_STEPS):
                step = width / (TPART + 1) ** (i + 1)
                dve.memset(steps[:, 0, i:i + 1], step).then_inc(dv, 1)
                dve.tensor_scalar(steps[:, 1, i:i + 1], pidx[:, 1:2], 1.0, step, ALU.add, ALU.mult).then_inc(dv, 1)
                n_own[0] += 2
            own(dve.memset(med[:, 0:1], SEARCH_FROM))
            dve.wait_ge(rt_in, 16)
            own(dve.tensor_copy(rhl[:, :, HI, :], rt[:, :, :]))
            dve.tensor_tensor(rhl[:, :, LO, :], rt[:, :, :], rhl[:, :, HI, :].bitcast(F32), ALU.subtract).then_inc(rhl_ready, 1)

            def token_stats(b):
                dve.wait_ge(x_in[b], 16)
                for h in range(2):
                    dve.bn_stats(bnst[:, h, :], x_sb[:, 2 * b + h, :]).then_inc(dv, 1)
                    n_own[0] += 1
                dve.wait_ge(dv, n_own[0])
                for h in range(2):
                    ins = dve.bn_aggr(mva[:, 2 * b + h, :], bnst[:, h, :])
                    if h == 0:
                        n_own[0] += 1
                        ins.then_inc(dv, 1)
                ins.then_inc(stats_a, 1)
                dve.wait_ge(dv, n_own[0])
                dve.wait_ge(stats_a, b + 1)

            def token_norm(b):
                dve.wait_ge(rstd_a, b + 1)
                for h in range(2):
                    if b >= 2:
                        dve.wait_ge(aT_ready, b - 1)
                    t = 2 * b + h
                    dve.tensor_scalar(aring[:, t % RING, :], x_sb[:, t, :], mva[:, t, 0:1], rsa[:, t:t + 1],
                                      ALU.subtract, ALU.mult).then_inc(a_ready, 1)

            def channel_stats(b):
                dve.wait_ge(aT_ready, b + 1)
                aT = GU[:, 2 * (b % 2):2 * (b % 2) + 2, :].rearrange("p a (h t) -> p (a h) t", t=TPB)
                for k in range(KC):
                    dve.bn_stats(bnst[:, k, :], aT[:, k, :]).then_inc(dv, 1)
                    n_own[0] += 1
                dve.wait_ge(dv, n_own[0])
                dve.tensor_reduce(U[:, b, :, MAX], aT, AX_X, ALU.max).then_inc(dv, 1)
                n_own[0] += 1
                for k in range(KC):
                    dve.bn_aggr(U[:, b, k, 0:2], bnst[:, k, :]).then_inc(dv, 1)
                    n_own[0] += 1
                dve.wait_ge(dv, n_own[0])
                dve.engine_nop().then_inc(chan_done, 1)

            token_stats(0)
            token_stats(1)
            token_norm(0)
            for b in range(1, B):
                if b + 1 < B:
                    token_stats(b + 1)
                token_norm(b)
                channel_stats(b - 1)
            channel_stats(B - 1)

            ub = scratch[:, 0:NV].rearrange("p (s b r) -> p s b r", s=KC * 3, b=B)
            dve.wait_ge(std_done, 1)
            Uf = U[:, :, :, :].rearrange("p b k s -> p b (k s)")
            dve.tensor_copy(ub, Uf.rearrange("p b s -> p s b").unsqueeze(3).to_broadcast([P, KC * 3, B, TPART])).then_inc(ub_ready, 1)
            V = GU[:, 0:3, :].rearrange("p a c -> p (a c)")
            dve.wait_ge(v_ready, 1)
            low, cnt, ind, thr, v1, c1, m2, cand = (med[:, i:i + 1] for i in range(8))
            junk = aring[:, 0:3, :].rearrange("p a c -> p (a c)")
            own(dve.tensor_tensor(thr, low, steps[:, 1, 0:1], ALU.add))
            for i in range(SEARCH_STEPS):
                own(dve.tensor_scalar(junk, V, thr, 0.0, ALU.is_le, ALU.add, accum_out=cnt))
                dve.tensor_scalar(ind, cnt, NV // 2 - 0.5, None, ALU.is_lt).then_inc(below, 1)
                dve.wait_ge(n_below, i + 1)
                own(dve.scalar_tensor_tensor(out=low, in0=yb[:, 0:1], scalar=steps[:, 0, i:i + 1], in1=low, op0=ALU.mult, op1=ALU.add))
                if i + 1 < SEARCH_STEPS:
                    own(dve.tensor_tensor(thr, low, steps[:, 1, i + 1:i + 2], ALU.add))
            pen = scratch[:, 0:NV]
            own(dve.tensor_scalar(pen, V, low, BIG, ALU.is_le, ALU.mult))
            own(dve.tensor_tensor_reduce(junk, V, pen, 1.0, 3e38, ALU.add, ALU.min, v1))
            own(dve.tensor_scalar(junk, V, v1, 0.0, ALU.is_le, ALU.add, accum_out=c1))
            own(dve.tensor_scalar(pen, V, v1, BIG, ALU.is_le, ALU.mult))
            own(dve.tensor_tensor_reduce(junk, V, pen, 1.0, 3e38, ALU.add, ALU.min, m2))
            own(dve.tensor_scalar(cand, c1, NV // 2 + 0.5, BIG, ALU.is_lt, ALU.mult))
            own(dve.tensor_tensor(cand, cand, v1, ALU.add))
            own(dve.tensor_tensor(m2, m2, cand, ALU.min))
            own(dve.tensor_tensor(m2, m2, v1, ALU.add))
            dve.tensor_scalar(medd[:, :], sel8[:, :], m2, 0.5, ALU.mult, ALU.mult).then_inc(medd_ready, 1)

            dve.wait_ge(med_b, 1)
            cw = par[:, 0:KC * 3].unsqueeze(1).to_broadcast([P, B, KC * 3])
            own(dve.tensor_tensor(U2[:, :, :], Uf, yb[:, 8:8 + B].unsqueeze(2).to_broadcast([P, B, KC * 3]), ALU.subtract))
            own(dve.tensor_tensor(Uf, U2[:, :, :], U2[:, :, :], ALU.mult))
            own(dve.tensor_tensor(Uf, Uf, U2[:, :, :], ALU.mult))
            dve.wait_ge(par_in, 16)
            own(dve.tensor_tensor(U2[:, :, :], Uf, cw, ALU.mult))
            own(dve.tensor_reduce(zt[:, :, :], U2[:, :, :].rearrange("p b (k s) -> p b k s", s=3), AX_X, ALU.add))
            bnw = par[:, 3 * KC:4 * KC].unsqueeze(1).to_broadcast([P, B, KC])
            bnb = par[:, 4 * KC:5 * KC].unsqueeze(1).to_broadcast([P, B, KC])
            own(dve.scalar_tensor_tensor(out=zt[:, :, :], in0=zt[:, :, :], scalar=-1.0 / (1.0 + BN_EPS) ** 0.5, in1=bnw, op0=ALU.mult, op1=ALU.mult))
            dve.tensor_tensor(zt[:, :, :], zt[:, :, :], bnb, ALU.subtract).then_inc(z_ready, 1)

            def gate_and_norm(t, u):
                buf, xt = aring[:, u, :], tile_of(x_sb, t)
                mean_a, r_a = mva[:, ds(t, 1), 0], rsa[:, ds(t, 1)]
                if not isinstance(t, int):
                    dve.wait_ge(xn_out[u], (t - u) * 4)
                    dve.wait_ge(tx_done, t - 3)
                dve.tensor_scalar(buf, xt, mean_a, r_a, ALU.subtract, ALU.mult).then_inc(t_norm, 1)
                dve.wait_ge(t_norm, t + 1)
                dve.wait_ge(gate_bc, half(t, u) + 1)
                dve.tensor_tensor(buf, buf, ms[:, :], ALU.mult).then_inc(gate_used, 1)
                dve.wait_ge(gate_used, t + 1)
                dve.tensor_tensor(buf, xt, buf, ALU.add).then_inc(t_x1, 1)
                dve.wait_ge(t_x1, t + 1)
                dve.bn_stats(bnst[:, 0, :], buf).then_inc(t_bn, 1)
                dve.wait_ge(z_ready, 1)
                dve.wait_ge(t_bn, t + 1)
                dve.bn_aggr(mvb[:, u, :], bnst[:, 0, :]).then_inc(stats_b, 1)
                dve.wait_ge(x1_kept, t + 1)
                dve.wait_ge(rstd_b, t + 1)
                dve.tensor_scalar(buf, buf, mvb[:, u, 0:1], rsb[:, u:u + 1], ALU.subtract, ALU.mult).then_inc(xn_ready, 1)

            def half(t, u):
                return t // 2 if isinstance(t, int) else batch_of[u]

            batch_of = [None] * RING

            def x_lo(n, slot):
                dve.wait_ge(xhi, n + 1)
                dve.tensor_tensor(xT[:, slot, LO, :, :], tx[:, :].rearrange("p (k t) -> p k t", k=KC),
                                  xT[:, slot, HI, :, :].bitcast(F32), ALU.subtract).then_inc(xlo, 1)

            def keep_logits(t, u):
                dve.wait_ge(logits, t + 1)
                dve.tensor_copy(lraw[:, t, :] if isinstance(t, int) else tile_of(lraw, t), th[:, 0:2 * E]).then_inc(logits_used, 1)

            def h_lo(n, parity):
                dve.wait_ge(hhi, n + 1)
                dve.tensor_tensor(hT[:, parity, LO, :, :], th[:, :].rearrange("p (k t) -> p k t", k=KC),
                                  hT[:, parity, HI, :, :].bitcast(F32), ALU.subtract).then_inc(hlo, 1)

            def gated(n, parity):
                dve.wait_ge(silu, n + 1)
                dve.wait_ge(u_done, n + 1)
                dve.tensor_tensor(sg[:, parity, :], sg[:, parity, :], gu(parity, UP), ALU.mult).then_inc(hid, 1)

            def add_shared(t):
                dve.wait_ge(y_done, t + 1)
                xt = tile_of(x_sb, t)
                dve.tensor_tensor(xt, xt, yb[:, :], ALU.add).then_inc(y_used, 1)

            for t in range(RING):
                gate_and_norm(t, t)
                if t:
                    x_lo(t - 1, t - 1)
                    keep_logits(t - 1, t - 1)
            x_lo(RING - 1, RING - 1)
            keep_logits(RING - 1, RING - 1)
            gated(0, 0)
            with dve.Fori(0, NT // RING - 1) as j:
                for u in range(RING):
                    n = j * RING + u
                    t = n + RING
                    batch_of[u] = j * 2 + (2 + u // 2)
                    gate_and_norm(t, u)
                    h_lo(n, u % 2)
                    gated(n + 1, (u + 1) % 2)
                    x_lo(t, u)
                    add_shared(n)
                    keep_logits(t, u)

            def temp(name_cols, *shape, dt=F32):
                a, b = name_cols
                v = rtmp[:, a:b]
                return v if dt == F32 else v.bitcast(dt)

            te = lambda v: v.rearrange("p (t e) -> p t e", e=E)
            L = te(rtmp[:, 0:128])
            score = te(rtmp[:, 128:256])
            mx = rtmp[:, 256:256 + NT]
            best = rtmp[:, 272:272 + NT]
            onehot = te(rtmp[:, 288:352].bitcast(BF16))
            rank = te(rtmp[:, 352:480])
            lflat = lraw[:, :, :].rearrange("p t e -> p (t e)")
            nblk, end, first = (lflat[:, i * E:(i + 1) * E] for i in range(3))
            first128 = rtmp[:, 504:512]
            cmp = rtmp[:, 512:640].rearrange("p (e t) -> p e t", e=E)
            slot = rtmp[:, 640:656]
            slot_i = rtmp[:, 656:688].bitcast(I32).rearrange("p (a t) -> p a t", a=2)
            slot_bj = rtmp[:, 688:720].rearrange("p (a t) -> p a t", a=2)
            nfield = 6
            field = rtmp[:, 720:720 + 48].bitcast(BF16).rearrange("p (t f) -> p t f", f=nfield)
            wrest = rtmp[:, 768:784]
            inblk = scratch[:, 0:NT * P // 2].bitcast(BF16).rearrange("p (t s) -> p t s", s=P)
            blk = rtmp[:, 784:784 + NT * NB // 2].bitcast(BF16).rearrange("p (t b) -> p t b", b=NB)
            sel = scratch[:, 1024:1024 + NT * nfield * NB // 2].bitcast(BF16).rearrange("p (t f b) -> p t f b", f=nfield, b=NB)
            inT = [P, NT, E]

            def choose():
                dve.wait_ge(logits_used, NT)
                own(dve.tensor_tensor(L, lraw[:, :, 0:E], lraw[:, :, E:2 * E], ALU.add))
                own(dve.tensor_reduce(mx, L, AX_X, ALU.max))
                dve.tensor_scalar(w_rt[:, :], mx, -1.0, None, ALU.mult).then_inc(w_ready, 1)
                own(dve.tensor_tensor(score, L, mx.unsqueeze(2).to_broadcast(inT), ALU.is_equal))
                rev = rev8[:, :].unsqueeze(1).to_broadcast(inT)
                own(dve.tensor_tensor(score, score, rev, ALU.mult))
                own(dve.tensor_reduce(best, score, AX_X, ALU.max))
                dve.tensor_tensor(onehot, best.unsqueeze(2).to_broadcast(inT), rev, ALU.is_equal).then_inc(onehot_ready, 1)

            def place():
                dve.wait_ge(rank_done, 1)
                counts = ms[:, 128:136].unsqueeze(2).to_broadcast([P, E, NT])
                own(dve.tensor_tensor(cmp, i128[:, :].unsqueeze(1).to_broadcast([P, E, NT]), counts, ALU.is_lt))
                own(dve.tensor_reduce(nblk, cmp, AX_X, ALU.add))
                own(dve.tensor_scalar(nblk, nblk, 1.0, None, ALU.max))
                own(dve.tensor_tensor_scan(end, ones[:, 0:E], nblk, 0.0, ALU.mult, ALU.add))
                own(dve.tensor_tensor(first, end, nblk, ALU.subtract))
                own(dve.tensor_scalar(first128, first, float(P), None, ALU.mult))
                own(dve.tensor_tensor(rank, te(ms[:, 0:128]), first128.unsqueeze(1).to_broadcast(inT), ALU.add))
                own(dve.tensor_tensor(rank, rank, onehot, ALU.mult))
                own(dve.tensor_reduce(slot, rank, AX_X, ALU.add))
                own(dve.tensor_copy(slot_i[:, 0, :], slot))
                own(dve.tensor_scalar(slot_i[:, 1, :], slot_i[:, 0, :], P - 1, None, ALU.bitwise_and))
                own(dve.tensor_scalar(slot_i[:, 0, :], slot_i[:, 0, :], P.bit_length() - 1, None, ALU.logical_shift_right))
                own(dve.tensor_copy(slot_bj, slot_i))
                dve.tensor_tensor(inblk, iota_f[:, :].unsqueeze(1).to_broadcast([P, NT, P]),
                                  slot_bj[:, 1, :].unsqueeze(2).to_broadcast([P, NT, P]), ALU.is_equal).then_inc(sel_ready, 1)
                own(dve.tensor_tensor(blk, iota_f[:, 0:NB].unsqueeze(1).to_broadcast([P, NT, NB]),
                                      slot_bj[:, 0, :].unsqueeze(2).to_broadcast([P, NT, NB]), ALU.is_equal))
                dve.wait_ge(w_ready, 2)
                own(dve.tensor_copy(field[:, :, 0], pidx[:, 0:1].to_broadcast([P, NT])))
                own(dve.tensor_copy(field[:, :, 1], i128[:, :]))
                own(dve.memset(field[:, :, 2], 1.0))
                own(dve.tensor_copy(field[:, :, 3], w_rt[:, :]))
                own(dve.tensor_tensor(wrest, w_rt[:, :], field[:, :, 3], ALU.subtract))
                own(dve.tensor_copy(field[:, :, 4], wrest))
                own(dve.tensor_tensor(wrest, wrest, field[:, :, 4], ALU.subtract))
                own(dve.tensor_copy(field[:, :, 5], wrest))
                for f in range(nfield):
                    dve.tensor_tensor(sel[:, :, f, :], blk, field[:, :, f].unsqueeze(2).to_broadcast([P, NT, NB]),
                                      ALU.mult).then_inc(sel_ready, 1)

            def slot_tables():
                dve.wait_ge(slots_done, 1)
                S = ms[:, 136:136 + nfield * NB].rearrange("p (f b) -> p f b", f=nfield)
                tok, row, wgt = (slotinfo[:, i, :] for i in range(3))
                own(dve.tensor_copy(tok, S[:, 0, :]))
                own(dve.tensor_tensor(tok, tok, S[:, 1, :], ALU.add))
                dve.tensor_copy(tokidx[:, :], tok).then_inc(slots_ready, 1)
                own(dve.tensor_scalar(row, S[:, 2, :], -2.0 * T, 2.0 * T, ALU.mult, ALU.add))
                own(dve.tensor_tensor(row, row, tok, ALU.add))
                dve.tensor_copy(scatidx[:, :], row).then_inc(slots_ready, 1)
                own(dve.tensor_copy(wgt, S[:, 5, :]))
                own(dve.tensor_tensor(wgt, wgt, S[:, 4, :], ALU.add))
                dve.tensor_tensor(wgt, wgt, S[:, 3, :], ALU.add).then_inc(slots_ready, 1)

            def block_table():
                be = [1, NB, E]
                o = [0]

                def t1(n):
                    o[0] += n
                    return scratch[0:1, o[0] - n:o[0]]

                c3 = t1(NB * E).rearrange("p (b e) -> p b e", e=E)
                oh = t1(NB * E).rearrange("p (b e) -> p b e", e=E)
                e_b, first_b, nblk_b, r_b, fl, odd, live = (t1(NB) for _ in range(7))
                ft = t1(NB * COLS).rearrange("p (b c) -> p b c", c=COLS)
                ei = t1(NB).bitcast(I32)
                row1 = lambda v: v[0:1, :]
                bidx = iota_f[0:1, 0:NB]
                own(dve.tensor_tensor(c3, row1(end).unsqueeze(1).to_broadcast(be), bidx.unsqueeze(2).to_broadcast(be), ALU.is_le))
                own(dve.tensor_reduce(e_b, c3, AX_X, ALU.add))
                own(dve.tensor_scalar(e_b, e_b, float(E - 1), None, ALU.min))
                own(dve.tensor_tensor(oh, iota_f[0:1, 0:E].unsqueeze(1).to_broadcast(be), e_b.unsqueeze(2).to_broadcast(be), ALU.is_equal))
                own(dve.tensor_tensor(c3, oh, row1(first).unsqueeze(1).to_broadcast(be), ALU.mult))
                own(dve.tensor_reduce(first_b, c3, AX_X, ALU.add))
                own(dve.tensor_tensor(c3, oh, row1(nblk).unsqueeze(1).to_broadcast(be), ALU.mult))
                own(dve.tensor_reduce(nblk_b, c3, AX_X, ALU.add))
                own(dve.tensor_tensor(r_b, bidx, first_b, ALU.subtract))
                own(dve.tensor_copy(ei, e_b))
                own(dve.tensor_scalar(ei, ei, 1, None, ALU.bitwise_and))
                own(dve.tensor_copy(odd, ei))
                own(dve.tensor_scalar(ft[:, :, SLOT_COL], odd, -1.0, 1.0, ALU.mult, ALU.add))
                own(dve.tensor_copy(ft[:, :, OTHER_COL], odd))
                own(dve.tensor_scalar(ft[:, :, READY_COL], e_b, 3.0, 3.0, ALU.mult, ALU.add))
                own(dve.tensor_scalar(ft[:, :, LOADED_COL], e_b, 16.0, 48.0, ALU.mult, ALU.add))
                own(dve.tensor_copy(ft[:, :, FIRST_COL], first_b))
                own(dve.tensor_scalar(live, e_b, float(E - 1), None, ALU.is_lt))
                own(dve.tensor_scalar(nblk_b, nblk_b, 1.0, None, ALU.subtract))
                for k in range(3):
                    own(dve.tensor_scalar(fl, nblk_b, float(k), None, ALU.min))
                    own(dve.tensor_tensor(fl, fl, r_b, ALU.is_equal))
                    own(dve.tensor_tensor(ft[:, :, FLAG_COL + k], fl, live, ALU.mult))
                dve.tensor_copy(tab[0:1, 0:NB, :], ft).then_inc(tables, 1)

            def next_set(c, ks, row):
                for k in ks:
                    with dve.If(row[FLAG_COL + k] > 0):
                        dve.wait_ge(whi, row[READY_COL] + (k + 4))
                        dve.wait_ge(wlo, row[READY_COL] + (k + 3))
                        out_q = ds(row[OTHER_COL], 1)
                        dve.tensor_tensor(wbuf[:, out_q, k, LO, :, :].rearrange("p a k c -> p (a k) c"), wraw[:, k, :, :],
                                          wbuf[:, out_q, k, HI, :, :].rearrange("p a k c -> p (a k) c").bitcast(F32),
                                          ALU.subtract).then_inc(wlo, 1)

            def add_routed(n, b, u, count):
                dve.wait_ge(y_done, n + 1)
                dve.wait_ge(zg_in[u], count)
                dve.scalar_tensor_tensor(out=zg[:, u, :], in0=yb[:, :], scalar=slotinfo[:, 2, ds(b, 1)], in1=zg[:, u, :],
                                         op0=ALU.mult, op1=ALU.add).then_inc(y_used, 1)

            for n in range(NT - RING, NT):
                i = n - (NT - RING)
                if i == 0:
                    choose()
                if i == 1:
                    place()
                if i == 2:
                    slot_tables()
                h_lo(n, n % 2)
                gated(n + 1, (n + 1) % 2)
                if n >= NT - 2:
                    x_lo(n + 2, n % 2)
                add_shared(n)
                if i == 2:
                    block_table()
            dve.wait_ge(tables, 1)
            next_set(0, range(3), table_row(dve, 0))
            with dve.Fori(0, (NB - 3) // 2) as j:
                for u in range(2):
                    n = j * 2 + (NT + u)
                    row = table_row(dve, j * 2 + (u + 1))
                    h_lo(n, u)
                    gated(n + 1, 1 - u)
                    x_lo(n + 2, u)
                    next_set(j * 2 + (u + 1), (GATE, UP), row)
                    add_routed(n, j * 2 + u, u, j * 16 + 16)
                    next_set(j * 2 + (u + 1), (DOWN,), row)
            for b in range(NB - 3, NB):
                n = NT + b
                h_lo(n, b % 2)
                if b + 1 < NB:
                    gated(n + 1, (b + 1) % 2)
                row = table_row(dve, b + 1) if b + 2 < NB else None
                if row:
                    x_lo(n + 2, b % 2)
                    next_set(b + 1, (GATE, UP), row)
                add_routed(n, b, b % 2, 16 * (b // 2 + 1))
                if row:
                    next_set(b + 1, (DOWN,), row)

        @block.tensor
        def _(pe):
            pe.wait_ge(consts, N_CONSTS)
            for b in range(B):
                if b >= 2:
                    pe.wait_ge(chan_done, b - 1)
                aT = GU[:, 2 * (b % 2):2 * (b % 2) + 2, :].rearrange("p a (h t) -> p (a h) t", t=TPB)
                for h in range(2):
                    t = 2 * b + h
                    pe.wait_ge(a_ready, t + 1)
                    for k in range(KC):
                        last = pe.transpose(aT[:, k, h * P:(h + 1) * P], aring[:, t % RING, k * P:(k + 1) * P], ident[:, :])
                last.then_inc(aT_ready, 1)
            ub = scratch[:, 0:NV].rearrange("p (s r) -> p s r", s=KC * 3)
            pe.wait_ge(ub_ready, 1)
            pe.wait_ge(chan_done, B)
            V = GU[:, 0:3, :].rearrange("p a c -> p (a c)")
            for s in range(KC * 3):
                last = pe.transpose(V[:, s * P:(s + 1) * P], ub[:, s, :], ident[:, :])
            last.then_inc(v_ready, 1)
            for i in range(SEARCH_STEPS):
                pe.wait_ge(below, i + 1)
                pe.matmul(yb[:, 0:1], bdiag[:, :, :].rearrange("p b r -> p (b r)"), med[:, 2:3], start=True, stop=True).then_inc(n_below, 1)
            pe.wait_ge(medd_ready, 1)
            pe.matmul(yb[:, 8:8 + B], ones[:, :], medd[:, :], start=True, stop=True).then_inc(med_b, 1)

            def spread_gate(b, u):
                pe.wait_ge(diag_ready, b + 1)
                if not (isinstance(b, int) and b == 0):
                    pe.wait_ge(gate_used, 2 * b if isinstance(b, int) else b * 2)
                pe.matmul(ms[:, :], ones[:, :], diag[:, u, :], start=True, stop=True).then_inc(gate_bc, 1)

            def transpose_x(n, src):
                if not (isinstance(n, int) and n == 0):
                    pe.wait_ge(xlo, n)
                for k in range(KC):
                    last = pe.transpose(tx[:, k * P:(k + 1) * P], src[:, k * P:(k + 1) * P], ident[:, :])
                last.then_inc(tx_done, 1)

            def transpose_h(n, parity):
                pe.wait_ge(hid, n + 1)
                if not (isinstance(n, int) and n == 0):
                    pe.wait_ge(hlo, n)
                for k in range(KC):
                    last = pe.transpose(th[:, k * P:(k + 1) * P], sg[:, parity, k * P:(k + 1) * P], ident[:, :])
                last.then_inc(th_done, 1)

            def product(dst, left, q, k):
                i = 0
                for kc in range(KC):
                    for lp, wp in ((HI, HI), (HI, LO), (LO, HI)):
                        last = pe.matmul(dst, left[:, lp, kc, :], wset(q, k, wp, kc), start=(i == 0), stop=(i == 3 * KC - 1))
                        i += 1
                return last

            def gate_product(n, slot, parity, q, before):
                pe.wait_ge(wlo, before + 1)
                pe.wait_ge(xlo, n + 1)
                product(gu(parity, GATE), xT[:, slot], q, GATE).then_inc(g_done, 1)

            def up_product(n, slot, parity, q, before):
                pe.wait_ge(wlo, before + 2)
                product(gu(parity, UP), xT[:, slot], q, UP).then_inc(u_done, 1)

            def down_product(n, parity, q, before):
                pe.wait_ge(wlo, before + 3)
                pe.wait_ge(hlo, n + 1)
                if not (isinstance(n, int) and n == 0):
                    pe.wait_ge(y_used, n)
                product(yb[:, :], hT[:, parity], q, DOWN).then_inc(y_done, 1)

            def route(t, slot):
                pe.wait_ge(xlo, t + 1)
                if not (isinstance(t, int) and t == 0):
                    pe.wait_ge(logits_used, t)
                for kc in range(KC):
                    for lp in (HI, LO):
                        last = pe.matmul(th[:, 0:2 * E], xT[:, slot, lp, kc, :], rhl[:, kc, :, :].rearrange("p h e -> p (h e)"),
                                         start=(kc == 0 and lp == HI), stop=(kc == KC - 1 and lp == LO))
                last.then_inc(logits, 1)

            pe.wait_ge(rhl_ready, 1)
            spread_gate(0, 0)
            for t in range(RING):
                pe.wait_ge(xn_ready, t + 1)
                if t == 1:
                    spread_gate(1, 1)
                if t == 3:
                    spread_gate(2, 0)
                transpose_x(t, aring[:, t, :])
                route(t, t)
            gate_product(0, 0, 0, 0, 0)
            up_product(0, 0, 0, 0, 0)
            with pe.Fori(0, NT // RING - 1) as j:
                for u in range(RING):
                    n = j * RING + u
                    gate_product(n + 1, (u + 1) % RING, (u + 1) % 2, 0, 0)
                    pe.wait_ge(logits_used, n + RING)
                    transpose_h(n, u % 2)
                    up_product(n + 1, (u + 1) % RING, (u + 1) % 2, 0, 0)
                    pe.wait_ge(xn_ready, n + RING + 1)
                    transpose_x(n + RING, aring[:, u, :])
                    if u % 2 == 1:
                        spread_gate(j * 2 + (3 + u // 2), (3 + u // 2) % 2)
                    down_product(n, u % 2, 0, 0)
                    route(n + RING, u)

            def rank():
                pe.wait_ge(onehot_ready, 1)
                oh = rtmp[:, 288:352].bitcast(BF16)
                pe.matmul(ms[:, 0:128], upper[:, :], oh, start=True, stop=False)
                for i in range(NT - 1):
                    pe.matmul(ms[:, (i + 1) * E:NT * E].rearrange("p (t e) -> p t e", e=E), ones_bf[:, :],
                              oh[:, i * E:(i + 1) * E].unsqueeze(1).to_broadcast([P, NT - 1 - i, E]),
                              start=False, stop=(i == NT - 2))
                for i in range(NT):
                    last = pe.matmul(ms[:, 128:136], ones_bf[:, :], oh[:, i * E:(i + 1) * E], start=(i == 0), stop=(i == NT - 1))
                last.then_inc(rank_done, 1)

            def fill_slots():
                nf = 6
                inblk = scratch[:, 0:NT * P // 2].bitcast(BF16).rearrange("p (t s) -> p t s", s=P)
                sel = scratch[:, 1024:1024 + NT * nf * NB // 2].bitcast(BF16).rearrange("p (t n) -> p t n", t=NT)
                pe.wait_ge(sel_ready, 1 + nf)
                for i in range(NT):
                    last = pe.matmul(ms[:, 136:136 + nf * NB], inblk[:, i, :], sel[:, i, :], start=(i == 0), stop=(i == NT - 1))
                last.then_inc(slots_done, 1)

            for n in range(NT - RING, NT):
                q, before = (0, 0) if n + 1 < NT else (1, 3)
                slot = (n + 1) % RING if n + 1 < NT else 0
                gate_product(n + 1, slot, (n + 1) % 2, q, before)
                pe.wait_ge(logits_used, NT)
                transpose_h(n, n % 2)
                up_product(n + 1, slot, (n + 1) % 2, q, before)
                if n == NT - RING:
                    rank()
                if n == NT - RING + 1:
                    fill_slots()
                if n >= NT - 2:
                    pe.wait_ge(xg_in[n % 2], 16)
                    transpose_x(n + 2, xg[:, n % 2, :])
                down_product(n, n % 2, 0, 0)

            def buffer_of(c):
                return (pe.value_load(tab[0:1, ds(c, 1), SLOT_COL], min_val=0, max_val=1),
                        pe.value_load(tab[0:1, ds(c, 1), READY_COL], min_val=0, max_val=3 * NSETS))

            pe.wait_ge(tables, 1)
            with pe.Fori(0, (NB - 3) // 2) as j:
                for u in range(2):
                    n = j * 2 + (NT + u)
                    q_next, before_next = buffer_of(j * 2 + (u + 1))
                    gate_product(n + 1, 1 - u, 1 - u, q_next, before_next)
                    transpose_h(n, u)
                    up_product(n + 1, 1 - u, 1 - u, q_next, before_next)
                    pe.wait_ge(xg_in[u], j * 16 + 32)
                    transpose_x(n + 2, xg[:, u, :])
                    q_this, before_this = buffer_of(j * 2 + u)
                    down_product(n, u, q_this, before_this)
            for b in range(NB - 3, NB):
                n = NT + b
                if b + 1 < NB:
                    q_next, before_next = buffer_of(b + 1)
                    gate_product(n + 1, (b + 1) % 2, (b + 1) % 2, q_next, before_next)
                transpose_h(n, b % 2)
                if b + 1 < NB:
                    up_product(n + 1, (b + 1) % 2, (b + 1) % 2, q_next, before_next)
                if b + 2 < NB:
                    pe.wait_ge(xg_in[b % 2], 16 * (b // 2 + 2))
                    transpose_x(n + 2, xg[:, b % 2, :])
                q_this, before_this = buffer_of(b)
                down_product(n, b % 2, q_this, before_this)


def kernel(x, L0_conv_cfc_w, L0_conv_bn_w, L0_conv_bn_b, L0_ffn_router_w, L0_ffn_w1, L0_ffn_v1, L0_ffn_w2,
           L0_ffn_shared_gate, L0_ffn_shared_up, L0_ffn_shared_down):
    import numpy as np
    import concourse.bacc as bacc
    from concourse.bass_utils import run_bass_kernel_spmd

    x = np.asarray(x)
    batch, chans, height, width = x.shape
    kc = chans // P

    def chunks(a):
        a = np.asarray(a).reshape(kc, P, -1)
        return np.ascontiguousarray(a.transpose(1, 0, 2)).reshape(P, -1)

    x_tok = np.ascontiguousarray(x.transpose(0, 2, 3, 1)).reshape(-1, chans)
    cfc = np.asarray(L0_conv_cfc_w)[:, [0, 2, 1]]
    conv_par = np.concatenate([chunks(cfc), chunks(L0_conv_bn_w), chunks(L0_conv_bn_b)], axis=1)
    router = chunks(np.asarray(L0_ffn_router_w).T)
    shared = [np.asarray(a).T for a in (L0_ffn_shared_gate, L0_ffn_shared_up, L0_ffn_shared_down)]
    sets = [shared] + [[np.asarray(a)[e] for a in (L0_ffn_w1, L0_ffn_v1, L0_ffn_w2)] for e in range(len(L0_ffn_w1))]
    weights = np.stack([np.stack([chunks(m) for m in one]) for one in sets])

    nc = bacc.Bacc("TRN2", target_bir_lowering=False, num_devices=1)
    arrays = {"x_tok": x_tok, "conv_par": conv_par, "router": router, "weights": weights}
    ins = [nc.dram_tensor(n, a.shape, F32, kind="ExternalInput").ap() for n, a in arrays.items()]
    xn_d = nc.dram_tensor("xn_d", x_tok.shape, F32).ap()
    z_d = nc.dram_tensor("z_d", x_tok.shape, F32).ap()
    out = nc.dram_tensor("out", x_tok.shape, F32, kind="ExternalOutput").ap()
    program(nc, *ins, xn_d, z_d, out)
    r = run_bass_kernel_spmd(nc, [arrays], core_ids=[0])
    got = r.results[0]["out"]
    return np.ascontiguousarray(got.reshape(batch, height, width, chans).transpose(0, 3, 1, 2))
```

```python
from contextlib import ExitStack

import concourse.bass as bass
from concourse import mybir

F32 = mybir.dt.float32
F32R = mybir.dt.float32r
BF16 = mybir.dt.bfloat16
I32 = mybir.dt.int32
U32 = mybir.dt.uint32
ALU = mybir.AluOpType
ACT = mybir.ActivationFunctionType
AX_X = mybir.AxisListType.X
ds = bass.ds

P = 128
LN_C_EPS = 1e-6
LN_T_EPS = 1e-5
BN_EPS = 1e-5
BIG = 1e30
MEAN, STD, MAX = range(3)
GATE, UP, DOWN = range(3)
HI, LO = range(2)
RING = 4
SEARCH_FROM, SEARCH_TO = -24.0, 24.0
SEARCH_STEPS = 7
N_CONSTS = 12
SLOT_COL, READY_COL, SLOT2_COL, READY2_COL = range(4)
MORE_COL, LAST_COL = 4, 5
OTHER_COL, FIRST_COL, LOADED_COL, BEFORE_COL = range(8, 12)
FLAG_COL, COLS = 12, 16


def program(nc, x_tok, conv_par, router, weights, xn_d, z_d, out):
    T, C = x_tok.shape
    B = 8
    TPB = T // B
    NT = T // P
    KC = C // P
    E = router.shape[1] // KC
    NSETS = weights.shape[0]
    NB = -(-(NT + E - 1) // RING) * RING
    NV = 3 * C
    TPART = P // B
    SURE = (NT - 1) // RING * RING
    assert C == 512 and KC == 4 and TPB == 2 * P and NSETS == E + 1 and E == 8

    with ExitStack() as ctx:
        def sb(name, shape, dt=F32):
            return ctx.enter_context(nc.sbuf_tensor(name, shape, dt))

        def ps(name, shape, dt=F32):
            return ctx.enter_context(nc.psum_tensor(name, shape, dt))

        def sem(name):
            return ctx.enter_context(nc.semaphore(name))

        x_sb = sb("x_sb", [P, NT, C])
        wbuf = sb("wbuf", [P, 2, 3, 2, KC, C], F32R)
        wraw = sb("wraw", [P, 3, KC, C])
        xT = sb("xT", [P, RING, 2, KC, P], F32R)
        aring = sb("aring", [P, RING, C])
        sg = sb("sg", [P, 2, C])
        hT = sb("hT", [P, 2, 2, KC, P], F32R)
        diag = sb("diag", [P, 2, C])
        scratch = sb("scratch", [P, 2176])
        xg = aring
        zg = x_sb[:, 0:RING, :]
        ident = sb("ident", [P, P])
        ones = sb("ones", [P, P])
        bdiag = sb("bdiag", [P, B, TPART])
        upper = sb("upper", [P, P], BF16)
        ones_bf = sb("ones_bf", [P, P], BF16)
        iota_f = sb("iota_f", [P, P])
        iota_i = scratch[:, 0:P].bitcast(I32)
        sel8 = sb("sel8", [P, B])
        pidx_i = sb("pidx_i", [P, 2], I32)
        pidx = sb("pidx", [P, 2])
        i128 = sb("i128", [P, NT])
        rev8 = sb("rev8", [P, E])
        par = sb("par", [P, KC * 5])
        rt = sb("rt", [P, KC, E])
        rhl = sb("rhl", [P, KC, 2, E], F32R)
        bnst = sb("bnst", [P, 4, 6])
        mva = sb("mva", [P, NT, 2])
        rsa = sb("rsa", [P, NT])
        mvb = sb("mvb", [P, RING, 2])
        rsb = sb("rsb", [P, RING])
        cpow = sb("cpow", [P, 4, B * KC])
        U = sb("U", [P, B, KC, 3])
        U2 = aring[:, 3, 0:B * KC * 3].rearrange("p (b s) -> p b s", b=B)
        steps = sb("steps", [P, 2, SEARCH_STEPS])
        med = sb("med", [P, 16])
        medd = sb("medd", [P, B])
        zt = sb("zt", [P, B, KC])
        g = sb("g", [P, B + 1, KC])
        lraw = sb("lraw", [P, NT, 2 * E])
        w_rt = sb("w_rt", [P, NT])
        tab = scratch[0:1, 1024:1024 + (NB + 1) * COLS].bitcast(I32).rearrange("p (b c) -> p b c", c=COLS)
        slotinfo = sb("slotinfo", [P, 3, NB])
        tokidx = sb("tokidx", [P, NB], U32)
        scatidx = sb("scatidx", [P, NB], U32)
        eps_t = sb("eps_t", [P, 1])

        rtmp = diag[:, :, :].rearrange("p a c -> p (a c)")

        GU = ps("GU", [P, 4, C])
        th = ps("th", [P, C])
        tx = ps("tx", [P, C])
        yb = ps("yb", [P, C])
        ms = ps("ms", [P, C])

        x_in = [sem(f"x_in{b}") for b in range(B)]
        par_in = sem("par_in")
        rt_in = sem("rt_in")
        w_in = [sem(f"w_in{k}") for k in range(3)]
        whi = sem("whi")
        wlo = sem("wlo")
        t_norm = sem("t_norm")
        t_gated = sem("t_gated")
        t_x1 = sem("t_x1")
        t_bn = sem("t_bn")
        t_eps = sem("t_eps")
        s_cnt = sem("s_cnt")
        s_low = sem("s_low")
        s_thr = sem("s_thr")
        iotas = sem("iotas")
        consts = sem("consts")
        dv = sem("dv")
        pl = sem("pl")
        stats_a = sem("stats_a")
        rstd_a = sem("rstd_a")
        a_ready = sem("a_ready")
        aT_ready = sem("aT_ready")
        chan_done = sem("chan_done")
        std_done = sem("std_done")
        ub_ready = sem("ub_ready")
        v_ready = sem("v_ready")
        below = sem("below")
        n_below = sem("n_below")
        medd_ready = sem("medd_ready")
        med_b = sem("med_b")
        z_ready = sem("z_ready")
        g_ready = sem("g_ready")
        diag_ready = sem("diag_ready")
        gate_bc = sem("gate_bc")
        gate_used = sem("gate_used")
        stats_b = sem("stats_b")
        rstd_b = sem("rstd_b")
        xn_ready = sem("xn_ready")
        xn_out = [sem(f"xn_out{u}") for u in range(RING)]
        tx_done = sem("tx_done")
        xhi = sem("xhi")
        xlo = sem("xlo")
        rhl_ready = sem("rhl_ready")
        logits = sem("logits")
        logits_used = sem("logits_used")
        g_done = sem("g_done")
        u_done = sem("u_done")
        silu = sem("silu")
        hid = sem("hid")
        th_done = sem("th_done")
        hhi = sem("hhi")
        hlo = sem("hlo")
        y_done = sem("y_done")
        y_used = sem("y_used")
        z_out = sem("z_out")
        onehot_ready = sem("onehot_ready")
        w_ready = sem("w_ready")
        rank_done = sem("rank_done")
        sel_ready = sem("sel_ready")
        slots_done = sem("slots_done")
        tables = sem("tables")
        slots_ready = sem("slots_ready")
        x1_kept = sem("x1_kept")
        xg_in = [sem(f"xg_in{u}") for u in range(RING)]
        zg_in = [sem(f"zg_in{u}") for u in range(RING)]
        o_out = [sem(f"o_out{u}") for u in range(RING)]

        block = ctx.enter_context(nc.Block())

        def gu(parity, which):
            return GU[:, 2 * parity + which, :]

        def wset(q, k, part, kc):
            if isinstance(q, int):
                return wbuf[:, q, k, part, kc, :]
            return wbuf[:, ds(q, 1), k, part, kc, :].rearrange("p a c -> p (a c)")

        def tile_of(buf, t):
            if isinstance(t, int):
                return buf[:, t, :]
            return buf[:, ds(t, 1), :].rearrange("p a c -> p (a c)")

        def table_entries(eng, c, cols):
            lowest = {READY_COL: 3, READY2_COL: 3, BEFORE_COL: 3, LOADED_COL: 48}
            highest = {READY_COL: 3 * NSETS, READY2_COL: 3 * NSETS, BEFORE_COL: 3 * NSETS, FIRST_COL: NB, LOADED_COL: 16 * (NSETS + 1)}
            row = tab[0:1, c:c + 1, cols.start:cols.stop] if isinstance(c, int) else tab[0:1, ds(c, 1), cols.start:cols.stop]
            _, got = nc.values_load_multi_w_load_instructions(row.rearrange("p b c -> p (b c)"), engines=[eng.engine])
            return [nc.s_assert_within(v, lowest.get(col, 0), highest.get(col, 1))
                    for v, col in zip(got, cols)]

        def groups(eng, step, last):
            with eng.Fori(0, SURE // RING) as j:
                for u in range(RING):
                    step(j * RING + u, u, j, 0)
            with eng.Fori(0, (NB - SURE) // RING) as j:
                for u in range(RING):
                    b = j * RING + (SURE + u)
                    more, final = table_entries(eng, b, range(MORE_COL, LAST_COL + 1))
                    with eng.If(more > 0):
                        step(b, u, j, SURE // RING)
                    with eng.If(final > 0):
                        last(b, u, j, SURE // RING)

        @block.sync
        def _(sp):
            def load_w(q, k):
                src = weights[q, k] if isinstance(q, int) else weights[ds(q, 1), k, :, :].rearrange("a p n -> (a p) n")
                sp.dma_start(wraw[:, k, :, :].rearrange("p k c -> p (k c)"), src).then_inc(w_in[k], 16)

            xv = x_tok.rearrange("(b t p) c -> b p t c", p=P, t=2)
            for b in range(B):
                sp.dma_start(x_sb[:, 2 * b:2 * b + 2, :], xv[b]).then_inc(x_in[b], 16)
            sp.dma_start(par[:, :], conv_par).then_inc(par_in, 16)
            sp.dma_start(rt[:, :, :], router.rearrange("p (k e) -> p k e", k=KC)).then_inc(rt_in, 16)
            for k in range(3):
                load_w(0, k)
            for k in range(3):
                sp.wait_ge(wlo, k + 1)
                load_w(1, k)

            def store_xn(t, u):
                sp.wait_ge(xn_ready, t + 1)
                sp.dma_start(xn_d[ds(t * P, P), :], aring[:, u, :]).then_inc(xn_out[u], 16)

            def store_z(t):
                sp.wait_ge(y_used, t + 1)
                sp.dma_start(z_d[ds(t * P, P), :], tile_of(x_sb, t)).then_inc(z_out, 16)

            for t in range(RING):
                store_xn(t, t)
            with sp.Fori(0, NT // RING - 1) as j:
                for u in range(RING):
                    store_xn(j * RING + (RING + u), u)
                    store_z(j * RING + u)
            for k in range(3):
                sp.wait_ge(wlo, 3 + k + 1)
                load_w(2, k)
            for t in range(NT - RING, NT):
                store_z(t)
            with sp.Fori(3, NSETS) as q:
                for k in range(3):
                    sp.wait_ge(wlo, q * 3 + (k - 2))
                    load_w(q, k)

        @block.gpsimd
        def _(pool):
            n_own = [0]

            def own(ins):
                n_own[0] += 1
                ins.then_inc(pl, 1)
                pool.wait_ge(pl, n_own[0])

            bk = lambda row: cpow[:, row, :].rearrange("p (b k) -> p b k", b=B)

            pool.iota(iota_i[:, :], pattern=[[1, P]], base=0, channel_multiplier=0).then_inc(iotas, 1)
            pool.iota(pidx_i[:, :], pattern=[[0, 2]], base=0, channel_multiplier=1).then_inc(iotas, 1)
            pool.memset(cpow[:, 0, :], -0.5).then_inc(consts, 1)
            pool.memset(cpow[:, 1, :], 0.5).then_inc(consts, 1)
            pool.memset(cpow[:, 2, :], -1.0).then_inc(consts, 1)
            pool.memset(cpow[:, 3, :], 2.718281828459045).then_inc(consts, 1)
            pool.memset(eps_t[:, :], LN_T_EPS).then_inc(consts, 1)
            pool.memset(ones[:, :], 1.0).then_inc(consts, 1)
            pool.memset(ones_bf[:, :], 1.0).then_inc(consts, 1)
            pool.memset(g[:, B, :], 0.0).then_inc(consts, 1)
            pool.memset(ident[:, :], 0.0).then_inc(pl, 1)
            pool.memset(sel8[:, :], 0.0).then_inc(pl, 1)
            pool.memset(bdiag[:, :, :], 1.0).then_inc(pl, 1)
            n_own[0] = 3
            own(pool.memset(upper[:, :], 1.0))
            pool.affine_select(out=ident[:, :], in_=ident[:, :], compare_op=ALU.not_equal, fill=1.0, base=0,
                               pattern=[[-1, P]], channel_multiplier=1).then_inc(consts, 1)
            pool.affine_select(out=sel8[:, :], in_=sel8[:, :], compare_op=ALU.not_equal, fill=1.0, base=0,
                               pattern=[[-TPART, B]], channel_multiplier=1).then_inc(consts, 1)
            pool.affine_select(out=upper[:, :], in_=upper[:, :], compare_op=ALU.is_gt, fill=0.0, base=0,
                               pattern=[[1, P]], channel_multiplier=-1).then_inc(consts, 1)
            own(pool.affine_select(out=bdiag[:, :, :], in_=bdiag[:, :, :], compare_op=ALU.is_ge, fill=0.0, base=0,
                                   pattern=[[-TPART, B], [0, TPART]], channel_multiplier=1))
            pool.affine_select(out=bdiag[:, :, :], in_=bdiag[:, :, :], compare_op=ALU.is_ge, fill=0.0,
                               base=TPART - 1, pattern=[[TPART, B], [0, TPART]], channel_multiplier=-1).then_inc(consts, 1)
            pool.wait_ge(consts, N_CONSTS)

            for b in range(B):
                pool.wait_ge(stats_a, b + 1)
                own(pool.tensor_scalar(rsa[:, 2 * b:2 * b + 2], mva[:, 2 * b:2 * b + 2, 1], LN_C_EPS, None, ALU.add))
                pool.tensor_tensor(rsa[:, 2 * b:2 * b + 2], rsa[:, 2 * b:2 * b + 2], cpow[:, 0, 0:2],
                                   ALU.pow).then_inc(rstd_a, 1)
            pool.wait_ge(chan_done, B)
            own(pool.tensor_scalar(zt[:, :, :], U[:, :, :, STD], float(TPB) / (TPB - 1), None, ALU.mult))
            pool.tensor_tensor(U[:, :, :, STD], zt[:, :, :], bk(1), ALU.pow).then_inc(std_done, 1)

            def split_lo(q, k, raw, hi, lo):
                pool.wait_ge(whi, 3 * q + k + 1)
                pool.tensor_tensor(lo, raw, hi.bitcast(F32), ALU.subtract).then_inc(wlo, 1)

            for k in range(3):
                split_lo(0, k, wraw[:, k, :, :], wbuf[:, 0, k, HI, :, :], wbuf[:, 0, k, LO, :, :])

            pool.wait_ge(z_ready, 1)
            own(pool.tensor_tensor(g[:, 0:B, :], bk(3), zt[:, :, :], ALU.pow))
            own(pool.tensor_scalar(g[:, 0:B, :], g[:, 0:B, :], 1.0, None, ALU.add))
            own(pool.tensor_tensor(g[:, 0:B, :], g[:, 0:B, :], bk(2), ALU.pow))

            def spread_diag(b, u):
                src = g[:, b, :] if isinstance(b, int) else g[:, ds(b, 1), :].rearrange("p a k -> p (a k)")
                pool.tensor_tensor(diag[:, u, :].rearrange("p (k c) -> p k c", k=KC),
                                   ident[:, :].unsqueeze(1).to_broadcast([P, KC, P]),
                                   src.unsqueeze(2).to_broadcast([P, KC, P]), ALU.mult).then_inc(diag_ready, 1)

            def rstd_tile(t, u):
                pool.wait_ge(stats_b, t + 1)
                r = rsb[:, u:u + 1]
                pool.tensor_tensor(r, mvb[:, u, 1:2], eps_t[:, 0:1], ALU.add).then_inc(t_eps, 1)
                pool.wait_ge(t_eps, t + 1)
                pool.tensor_tensor(r, r, cpow[:, 0, 0:1], ALU.pow).then_inc(rstd_b, 1)

            spread_diag(0, 0)
            spread_diag(1, 1)
            rstd_tile(0, 0)
            rstd_tile(1, 1)
            spread_diag(2, 0)
            rstd_tile(2, 2)
            rstd_tile(3, 3)
            with pool.Fori(0, NT // RING - 1) as j:
                for u in range(RING):
                    rstd_tile(j * RING + (RING + u), u)
                    if u % 2 == 1:
                        spread_diag(j * 2 + (3 + u // 2), (3 + u // 2) % 2)

            def split_set_1(k):
                split_lo(1, k, wraw[:, k, :, :], wbuf[:, 1, k, HI, :, :], wbuf[:, 1, k, LO, :, :])

            split_set_1(GATE)
            pool.wait_ge(w_ready, 1)
            own(pool.tensor_tensor(w_rt[:, :], cpow[:, 3, 0:NT], w_rt[:, :], ALU.pow))
            own(pool.tensor_scalar(w_rt[:, :], w_rt[:, :], 1.0, None, ALU.add))
            pool.tensor_tensor(w_rt[:, :], w_rt[:, :], cpow[:, 2, 0:NT], ALU.pow).then_inc(w_ready, 1)
            split_set_1(UP)

            def rows(table, b):
                return bass.IndirectOffsetOnAxis(ap=table[:, b:b + 1], axis=0)

            def gather_x(b):
                pool.indirect_dma_start(xg[:, b % RING, :], None, xn_d[:, :], rows(tokidx, b)).then_inc(xg_in[b % RING], 16)

            def gather_z(b):
                pool.indirect_dma_start(zg[:, b % RING, :], None, z_d[:, :], rows(tokidx, b)).then_inc(zg_in[b % RING], 16)

            def scatter(b):
                pool.wait_ge(y_used, NT + b + 1)
                pool.indirect_dma_start(out[:, :], rows(scatidx, b), zg[:, b % RING, :], None,
                                        bounds_check=T - 1, oob_is_err=False).then_inc(o_out[b % RING], 16)

            def stored(b):
                pool.wait_ge(o_out[b % RING], 16 * (b // RING + 1))

            pool.wait_ge(slots_ready, 3)
            for u in range(RING):
                pool.wait_ge(xn_out[u], 16 * (NT // RING))
            pool.wait_ge(tx_done, NT)
            for b in range(RING):
                gather_x(b)
            split_set_1(DOWN)
            pool.wait_ge(z_out, 16 * NT)
            for b in range(RING - 1):
                gather_z(b)
            pool.wait_ge(tables, 1)

            def fetch_x(b):
                pool.wait_ge(tx_done, NT + b - RING + 1)
                gather_x(b)

            for b in range(NB):
                c = b + RING - 1
                if c + 1 < NT:
                    fetch_x(c + 1)
                    scatter(b)
                    if b:
                        stored(b - 1)
                    gather_z(c)
                    continue
                needed = table_entries(pool, c - 1, range(MORE_COL, MORE_COL + 1))[0] if c < NB else None
                if c + 1 < NB:
                    with pool.If(needed > 0):
                        fetch_x(c + 1)
                here, = table_entries(pool, b - 1, range(MORE_COL, MORE_COL + 1))
                with pool.If(here > 0):
                    scatter(b)
                    stored(b - 1)
                if c < NB:
                    with pool.If(needed > 0):
                        gather_z(c)
                with pool.If(table_entries(pool, b, range(LAST_COL, LAST_COL + 1))[0] > 0):
                    stored(b)

        @block.scalar
        def _(act):
            def split_hi(raw, hi):
                act.activation(hi, raw, ACT.Copy).then_inc(whi, 1)

            for q in range(2):
                for k in range(3):
                    act.wait_ge(w_in[k], 16 * (q + 1))
                    split_hi(wraw[:, k, :, :], wbuf[:, q, k, HI, :, :])

            def x_hi(n, slot):
                act.wait_ge(tx_done, n + 1)
                act.activation(xT[:, slot, HI, :, :], tx[:, :].rearrange("p (k t) -> p k t", k=KC), ACT.Copy).then_inc(xhi, 1)

            def silu_gate(n, parity):
                act.wait_ge(g_done, n + 1)
                act.activation(sg[:, parity, :], gu(parity, GATE), ACT.Silu).then_inc(silu, 1)

            def h_hi(n, parity):
                act.wait_ge(th_done, n + 1)
                act.activation(hT[:, parity, HI, :, :], th[:, :].rearrange("p (k t) -> p k t", k=KC), ACT.Copy).then_inc(hhi, 1)

            def keep_x1(t, u):
                act.wait_ge(t_x1, t + 1)
                act.activation(tile_of(x_sb, t), aring[:, u, :], ACT.Copy).then_inc(x1_kept, 1)

            for t in range(RING):
                keep_x1(t, t)
                x_hi(t, t)
            silu_gate(0, 0)
            with act.Fori(0, NT // RING - 1) as j:
                for u in range(RING):
                    n = j * RING + u
                    keep_x1(n + RING, u)
                    h_hi(n, u % 2)
                    silu_gate(n + 1, (u + 1) % 2)
                    x_hi(n + RING, u)
            for n in range(NT - RING, NT):
                h_hi(n, n % 2)
                silu_gate(n + 1, (n + 1) % 2)
                if n >= NT - 2:
                    x_hi(n + 2, n % 2)

            def next_set(c):
                due = table_entries(act, c, range(FLAG_COL, FLAG_COL + 3))
                for k in range(3):
                    with act.If(due[k] > 0):
                        other, first, loaded = table_entries(act, c, range(OTHER_COL, LOADED_COL + 1))
                        act.wait_ge(w_in[k], loaded)
                        act.wait_ge(y_done if k == DOWN else u_done, first + NT)
                        split_hi(wraw[:, k, :, :], wbuf[:, ds(other, 1), k, HI, :, :].rearrange("p a k c -> p (a k) c"))

            def step(b, u, j, base):
                h_hi(b + NT, u % 2)
                silu_gate(b + (NT + 1), 1 - u % 2)
                x_hi(b + (NT + 2), u % 2)
                next_set(b + 1)

            def last(b, u, j, base):
                h_hi(b + NT, u % 2)

            act.wait_ge(tables, 1)
            next_set(0)
            groups(act, step, last)

        @block.vector
        def _(dve):
            n_own = [0]

            def own(ins):
                n_own[0] += 1
                ins.then_inc(dv, 1)
                dve.wait_ge(dv, n_own[0])

            dve.wait_ge(iotas, 2)
            dve.tensor_scalar(pidx_i[:, 1:2], pidx_i[:, 1:2], TPART - 1, None, ALU.bitwise_and).then_inc(dv, 1)
            n_own[0] += 1
            own(dve.tensor_copy(iota_f[:, :], iota_i[:, :]))
            own(dve.tensor_copy(pidx[:, :], pidx_i[:, :]))
            dve.tensor_scalar(i128[:, :], iota_f[:, 0:NT], float(P), None, ALU.mult).then_inc(dv, 1)
            dve.tensor_scalar(rev8[:, :], iota_f[:, 0:E], -1.0, float(E), ALU.mult, ALU.add).then_inc(dv, 1)
            n_own[0] += 2
            width = SEARCH_TO - SEARCH_FROM
            for i in range(SEARCH_STEPS):
                step = width / (TPART + 1) ** (i + 1)
                dve.memset(steps[:, 0, i:i + 1], step).then_inc(dv, 1)
                dve.tensor_scalar(steps[:, 1, i:i + 1], pidx[:, 1:2], 1.0, step, ALU.add, ALU.mult).then_inc(dv, 1)
                n_own[0] += 2
            own(dve.memset(med[:, 0:1], SEARCH_FROM))
            dve.wait_ge(rt_in, 16)
            own(dve.tensor_copy(rhl[:, :, HI, :], rt[:, :, :]))
            dve.tensor_tensor(rhl[:, :, LO, :], rt[:, :, :], rhl[:, :, HI, :].bitcast(F32), ALU.subtract).then_inc(rhl_ready, 1)

            def token_stats(b):
                dve.wait_ge(x_in[b], 16)
                for h in range(2):
                    dve.bn_stats(bnst[:, h, :], x_sb[:, 2 * b + h, :]).then_inc(dv, 1)
                    n_own[0] += 1
                dve.wait_ge(dv, n_own[0])
                for h in range(2):
                    ins = dve.bn_aggr(mva[:, 2 * b + h, :], bnst[:, h, :])
                    if h == 0:
                        n_own[0] += 1
                        ins.then_inc(dv, 1)
                ins.then_inc(stats_a, 1)
                dve.wait_ge(dv, n_own[0])
                dve.wait_ge(stats_a, b + 1)

            def token_norm(b):
                dve.wait_ge(rstd_a, b + 1)
                for h in range(2):
                    if b >= 2:
                        dve.wait_ge(aT_ready, b - 1)
                    t = 2 * b + h
                    dve.tensor_scalar(aring[:, t % RING, :], x_sb[:, t, :], mva[:, t, 0:1], rsa[:, t:t + 1],
                                      ALU.subtract, ALU.mult).then_inc(a_ready, 1)

            def channel_stats(b):
                dve.wait_ge(aT_ready, b + 1)
                aT = GU[:, 2 * (b % 2):2 * (b % 2) + 2, :].rearrange("p a (h t) -> p (a h) t", t=TPB)
                for k in range(KC):
                    dve.bn_stats(bnst[:, k, :], aT[:, k, :]).then_inc(dv, 1)
                    n_own[0] += 1
                dve.wait_ge(dv, n_own[0])
                dve.tensor_reduce(U[:, b, :, MAX], aT, AX_X, ALU.max).then_inc(dv, 1)
                n_own[0] += 1
                for k in range(KC):
                    dve.bn_aggr(U[:, b, k, 0:2], bnst[:, k, :]).then_inc(dv, 1)
                    n_own[0] += 1
                dve.wait_ge(dv, n_own[0])
                dve.engine_nop().then_inc(chan_done, 1)

            token_stats(0)
            token_stats(1)
            token_norm(0)
            for b in range(1, B):
                if b + 1 < B:
                    token_stats(b + 1)
                token_norm(b)
                channel_stats(b - 1)
            channel_stats(B - 1)

            ub = scratch[:, 0:NV].rearrange("p (s b r) -> p s b r", s=KC * 3, b=B)
            dve.wait_ge(std_done, 1)
            Uf = U[:, :, :, :].rearrange("p b k s -> p b (k s)")
            dve.tensor_copy(ub, Uf.rearrange("p b s -> p s b").unsqueeze(3).to_broadcast([P, KC * 3, B, TPART])).then_inc(ub_ready, 1)
            V = GU[:, 0:3, :].rearrange("p a c -> p (a c)")
            dve.wait_ge(v_ready, 1)
            low, cnt, ind, thr, v1, c1, m2, cand = (med[:, i:i + 1] for i in range(8))
            junk = aring[:, 0:3, :].rearrange("p a c -> p (a c)")
            own(dve.tensor_tensor(thr, low, steps[:, 1, 0:1], ALU.add))
            for i in range(SEARCH_STEPS):
                own(dve.tensor_scalar(junk, V, thr, 0.0, ALU.is_le, ALU.add, accum_out=cnt))
                dve.tensor_scalar(ind, cnt, NV // 2 - 0.5, None, ALU.is_lt).then_inc(below, 1)
                dve.wait_ge(n_below, i + 1)
                own(dve.scalar_tensor_tensor(out=low, in0=yb[:, 0:1], scalar=steps[:, 0, i:i + 1], in1=low, op0=ALU.mult, op1=ALU.add))
                if i + 1 < SEARCH_STEPS:
                    own(dve.tensor_tensor(thr, low, steps[:, 1, i + 1:i + 2], ALU.add))
            pen = scratch[:, 0:NV]
            own(dve.tensor_scalar(pen, V, low, BIG, ALU.is_le, ALU.mult))
            own(dve.tensor_tensor_reduce(junk, V, pen, 1.0, 3e38, ALU.add, ALU.min, v1))
            own(dve.tensor_scalar(junk, V, v1, 0.0, ALU.is_le, ALU.add, accum_out=c1))
            own(dve.tensor_scalar(pen, V, v1, BIG, ALU.is_le, ALU.mult))
            own(dve.tensor_tensor_reduce(junk, V, pen, 1.0, 3e38, ALU.add, ALU.min, m2))
            own(dve.tensor_scalar(cand, c1, NV // 2 + 0.5, BIG, ALU.is_lt, ALU.mult))
            own(dve.tensor_tensor(cand, cand, v1, ALU.add))
            own(dve.tensor_tensor(m2, m2, cand, ALU.min))
            own(dve.tensor_tensor(m2, m2, v1, ALU.add))
            dve.tensor_scalar(medd[:, :], sel8[:, :], m2, 0.5, ALU.mult, ALU.mult).then_inc(medd_ready, 1)

            dve.wait_ge(med_b, 1)
            cw = par[:, 0:KC * 3].unsqueeze(1).to_broadcast([P, B, KC * 3])
            own(dve.tensor_tensor(U2[:, :, :], Uf, yb[:, 8:8 + B].unsqueeze(2).to_broadcast([P, B, KC * 3]), ALU.subtract))
            own(dve.tensor_tensor(Uf, U2[:, :, :], U2[:, :, :], ALU.mult))
            own(dve.tensor_tensor(Uf, Uf, U2[:, :, :], ALU.mult))
            dve.wait_ge(par_in, 16)
            own(dve.tensor_tensor(U2[:, :, :], Uf, cw, ALU.mult))
            own(dve.tensor_reduce(zt[:, :, :], U2[:, :, :].rearrange("p b (k s) -> p b k s", s=3), AX_X, ALU.add))
            bnw = par[:, 3 * KC:4 * KC].unsqueeze(1).to_broadcast([P, B, KC])
            bnb = par[:, 4 * KC:5 * KC].unsqueeze(1).to_broadcast([P, B, KC])
            own(dve.scalar_tensor_tensor(out=zt[:, :, :], in0=zt[:, :, :], scalar=-1.0 / (1.0 + BN_EPS) ** 0.5, in1=bnw, op0=ALU.mult, op1=ALU.mult))
            dve.tensor_tensor(zt[:, :, :], zt[:, :, :], bnb, ALU.subtract).then_inc(z_ready, 1)

            def gate_and_norm(t, u):
                buf, xt = aring[:, u, :], tile_of(x_sb, t)
                mean_a, r_a = mva[:, ds(t, 1), 0], rsa[:, ds(t, 1)]
                if not isinstance(t, int):
                    dve.wait_ge(xn_out[u], (t - u) * 4)
                    dve.wait_ge(tx_done, t - 3)
                dve.tensor_scalar(buf, xt, mean_a, r_a, ALU.subtract, ALU.mult).then_inc(t_norm, 1)
                dve.wait_ge(t_norm, t + 1)
                dve.wait_ge(gate_bc, half(t, u) + 1)
                dve.tensor_tensor(buf, buf, ms[:, :], ALU.mult).then_inc(gate_used, 1)
                dve.wait_ge(gate_used, t + 1)
                dve.tensor_tensor(buf, xt, buf, ALU.add).then_inc(t_x1, 1)
                dve.wait_ge(t_x1, t + 1)
                dve.bn_stats(bnst[:, 0, :], buf).then_inc(t_bn, 1)
                dve.wait_ge(z_ready, 1)
                dve.wait_ge(t_bn, t + 1)
                dve.bn_aggr(mvb[:, u, :], bnst[:, 0, :]).then_inc(stats_b, 1)
                dve.wait_ge(x1_kept, t + 1)
                dve.wait_ge(rstd_b, t + 1)
                dve.tensor_scalar(buf, buf, mvb[:, u, 0:1], rsb[:, u:u + 1], ALU.subtract, ALU.mult).then_inc(xn_ready, 1)

            def half(t, u):
                return t // 2 if isinstance(t, int) else batch_of[u]

            batch_of = [None] * RING

            def x_lo(n, slot):
                dve.wait_ge(xhi, n + 1)
                dve.tensor_tensor(xT[:, slot, LO, :, :], tx[:, :].rearrange("p (k t) -> p k t", k=KC),
                                  xT[:, slot, HI, :, :].bitcast(F32), ALU.subtract).then_inc(xlo, 1)

            def keep_logits(t, u):
                dve.wait_ge(logits, t + 1)
                dve.tensor_copy(lraw[:, t, :] if isinstance(t, int) else tile_of(lraw, t), th[:, 0:2 * E]).then_inc(logits_used, 1)

            def h_lo(n, parity):
                dve.wait_ge(hhi, n + 1)
                dve.tensor_tensor(hT[:, parity, LO, :, :], th[:, :].rearrange("p (k t) -> p k t", k=KC),
                                  hT[:, parity, HI, :, :].bitcast(F32), ALU.subtract).then_inc(hlo, 1)

            def gated(n, parity):
                dve.wait_ge(silu, n + 1)
                dve.wait_ge(u_done, n + 1)
                dve.tensor_tensor(sg[:, parity, :], sg[:, parity, :], gu(parity, UP), ALU.mult).then_inc(hid, 1)

            def add_shared(t):
                dve.wait_ge(y_done, t + 1)
                xt = tile_of(x_sb, t)
                dve.tensor_tensor(xt, xt, yb[:, :], ALU.add).then_inc(y_used, 1)

            for t in range(RING):
                gate_and_norm(t, t)
                if t:
                    x_lo(t - 1, t - 1)
                    keep_logits(t - 1, t - 1)
            x_lo(RING - 1, RING - 1)
            keep_logits(RING - 1, RING - 1)
            gated(0, 0)
            with dve.Fori(0, NT // RING - 1) as j:
                for u in range(RING):
                    n = j * RING + u
                    t = n + RING
                    batch_of[u] = j * 2 + (2 + u // 2)
                    gate_and_norm(t, u)
                    h_lo(n, u % 2)
                    gated(n + 1, (u + 1) % 2)
                    x_lo(t, u)
                    add_shared(n)
                    keep_logits(t, u)

            def temp(name_cols, *shape, dt=F32):
                a, b = name_cols
                v = rtmp[:, a:b]
                return v if dt == F32 else v.bitcast(dt)

            te = lambda v: v.rearrange("p (t e) -> p t e", e=E)
            L = te(rtmp[:, 0:128])
            score = te(rtmp[:, 128:256])
            mx = rtmp[:, 256:256 + NT]
            best = rtmp[:, 272:272 + NT]
            onehot = te(rtmp[:, 288:352].bitcast(BF16))
            rank = te(rtmp[:, 352:480])
            nblk, end, first = (rtmp[:, 480 + i * E:480 + (i + 1) * E] for i in range(3))
            first128 = rtmp[:, 504:512]
            cmp = rtmp[:, 512:640].rearrange("p (e t) -> p e t", e=E)
            slot = rtmp[:, 640:656]
            slot_i = rtmp[:, 656:688].bitcast(I32).rearrange("p (a t) -> p a t", a=2)
            slot_bj = rtmp[:, 688:720].rearrange("p (a t) -> p a t", a=2)
            nfield = 6
            field = rtmp[:, 720:720 + 48].bitcast(BF16).rearrange("p (t f) -> p t f", f=nfield)
            wrest = rtmp[:, 768:784]
            inblk = scratch[:, 0:NT * P // 2].bitcast(BF16).rearrange("p (t s) -> p t s", s=P)
            blk = rtmp[:, 784:784 + NT * NB // 2].bitcast(BF16).rearrange("p (t b) -> p t b", b=NB)
            sel = scratch[:, 1024:1024 + NT * nfield * NB // 2].bitcast(BF16).rearrange("p (t f b) -> p t f b", f=nfield, b=NB)
            inT = [P, NT, E]

            def choose():
                dve.wait_ge(logits_used, NT)
                own(dve.tensor_tensor(L, lraw[:, :, 0:E], lraw[:, :, E:2 * E], ALU.add))
                own(dve.tensor_reduce(mx, L, AX_X, ALU.max))
                dve.tensor_scalar(w_rt[:, :], mx, -1.0, None, ALU.mult).then_inc(w_ready, 1)
                own(dve.tensor_tensor(score, L, mx.unsqueeze(2).to_broadcast(inT), ALU.is_equal))
                rev = rev8[:, :].unsqueeze(1).to_broadcast(inT)
                own(dve.tensor_tensor(score, score, rev, ALU.mult))
                own(dve.tensor_reduce(best, score, AX_X, ALU.max))
                dve.tensor_tensor(onehot, best.unsqueeze(2).to_broadcast(inT), rev, ALU.is_equal).then_inc(onehot_ready, 1)

            def place():
                dve.wait_ge(rank_done, 1)
                counts = ms[:, 128:136].unsqueeze(2).to_broadcast([P, E, NT])
                own(dve.tensor_tensor(cmp, i128[:, :].unsqueeze(1).to_broadcast([P, E, NT]), counts, ALU.is_lt))
                own(dve.tensor_reduce(nblk, cmp, AX_X, ALU.add))
                own(dve.tensor_scalar(nblk, nblk, 1.0, None, ALU.max))
                own(dve.tensor_tensor_scan(end, ones[:, 0:E], nblk, 0.0, ALU.mult, ALU.add))
                own(dve.tensor_tensor(first, end, nblk, ALU.subtract))
                own(dve.tensor_scalar(first128, first, float(P), None, ALU.mult))
                own(dve.tensor_tensor(rank, te(ms[:, 0:128]), first128.unsqueeze(1).to_broadcast(inT), ALU.add))
                own(dve.tensor_tensor(rank, rank, onehot, ALU.mult))
                own(dve.tensor_reduce(slot, rank, AX_X, ALU.add))
                own(dve.tensor_copy(slot_i[:, 0, :], slot))
                own(dve.tensor_scalar(slot_i[:, 1, :], slot_i[:, 0, :], P - 1, None, ALU.bitwise_and))
                own(dve.tensor_scalar(slot_i[:, 0, :], slot_i[:, 0, :], P.bit_length() - 1, None, ALU.logical_shift_right))
                own(dve.tensor_copy(slot_bj, slot_i))
                dve.tensor_tensor(inblk, iota_f[:, :].unsqueeze(1).to_broadcast([P, NT, P]),
                                  slot_bj[:, 1, :].unsqueeze(2).to_broadcast([P, NT, P]), ALU.is_equal).then_inc(sel_ready, 1)
                own(dve.tensor_tensor(blk, iota_f[:, 0:NB].unsqueeze(1).to_broadcast([P, NT, NB]),
                                      slot_bj[:, 0, :].unsqueeze(2).to_broadcast([P, NT, NB]), ALU.is_equal))
                dve.wait_ge(w_ready, 2)
                own(dve.tensor_copy(field[:, :, 0], pidx[:, 0:1].to_broadcast([P, NT])))
                own(dve.tensor_copy(field[:, :, 1], i128[:, :]))
                own(dve.memset(field[:, :, 2], 1.0))
                own(dve.tensor_copy(field[:, :, 3], w_rt[:, :]))
                own(dve.tensor_tensor(wrest, w_rt[:, :], field[:, :, 3], ALU.subtract))
                own(dve.tensor_copy(field[:, :, 4], wrest))
                own(dve.tensor_tensor(wrest, wrest, field[:, :, 4], ALU.subtract))
                own(dve.tensor_copy(field[:, :, 5], wrest))
                for f in range(nfield):
                    dve.tensor_tensor(sel[:, :, f, :], blk, field[:, :, f].unsqueeze(2).to_broadcast([P, NT, NB]),
                                      ALU.mult).then_inc(sel_ready, 1)

            def slot_tables():
                dve.wait_ge(slots_done, 1)
                S = ms[:, 136:136 + nfield * NB].rearrange("p (f b) -> p f b", f=nfield)
                tok, row, wgt = (slotinfo[:, i, :] for i in range(3))
                own(dve.tensor_copy(tok, S[:, 0, :]))
                own(dve.tensor_tensor(tok, tok, S[:, 1, :], ALU.add))
                dve.tensor_copy(tokidx[:, :], tok).then_inc(slots_ready, 1)
                own(dve.tensor_scalar(row, S[:, 2, :], -2.0 * T, 2.0 * T, ALU.mult, ALU.add))
                own(dve.tensor_tensor(row, row, tok, ALU.add))
                dve.tensor_copy(scatidx[:, :], row).then_inc(slots_ready, 1)
                own(dve.tensor_copy(wgt, S[:, 5, :]))
                own(dve.tensor_tensor(wgt, wgt, S[:, 4, :], ALU.add))
                dve.tensor_tensor(wgt, wgt, S[:, 3, :], ALU.add).then_inc(slots_ready, 1)

            def block_table():
                be = [1, NB, E]
                o = [0]

                def t1(n):
                    o[0] += n
                    return scratch[0:1, o[0] - n:o[0]]

                c3 = t1(NB * E).rearrange("p (b e) -> p b e", e=E)
                oh = t1(NB * E).rearrange("p (b e) -> p b e", e=E)
                e_b, first_b, nblk_b, r_b, fl, odd, live, after = (t1(NB) for _ in range(8))
                ft = t1(NB * COLS).rearrange("p (b c) -> p b c", c=COLS)
                ei = t1(NB).bitcast(I32)
                row1 = lambda v: v[0:1, :]
                bidx = iota_f[0:1, 0:NB]
                own(dve.tensor_tensor(c3, row1(end).unsqueeze(1).to_broadcast(be), bidx.unsqueeze(2).to_broadcast(be), ALU.is_le))
                own(dve.tensor_reduce(e_b, c3, AX_X, ALU.add))
                own(dve.tensor_scalar(e_b, e_b, float(E - 1), None, ALU.min))
                own(dve.tensor_tensor(oh, iota_f[0:1, 0:E].unsqueeze(1).to_broadcast(be), e_b.unsqueeze(2).to_broadcast(be), ALU.is_equal))
                own(dve.tensor_tensor(c3, oh, row1(first).unsqueeze(1).to_broadcast(be), ALU.mult))
                own(dve.tensor_reduce(first_b, c3, AX_X, ALU.add))
                own(dve.tensor_tensor(c3, oh, row1(nblk).unsqueeze(1).to_broadcast(be), ALU.mult))
                own(dve.tensor_reduce(nblk_b, c3, AX_X, ALU.add))
                own(dve.tensor_tensor(r_b, bidx, first_b, ALU.subtract))
                own(dve.tensor_copy(ei, e_b))
                own(dve.tensor_scalar(ei, ei, 1, None, ALU.bitwise_and))
                own(dve.tensor_copy(odd, ei))
                own(dve.tensor_scalar(ft[:, :, SLOT_COL], odd, -1.0, 1.0, ALU.mult, ALU.add))
                own(dve.tensor_copy(ft[:, :, OTHER_COL], odd))
                own(dve.tensor_scalar(ft[:, :, READY_COL], e_b, 3.0, 3.0, ALU.mult, ALU.add))
                own(dve.tensor_copy(ft[:, :, BEFORE_COL], ft[:, :, READY_COL]))
                own(dve.tensor_copy(ft[:, 0:NB - 1, SLOT2_COL:READY2_COL + 1], ft[:, 1:NB, SLOT_COL:READY_COL + 1]))
                own(dve.tensor_copy(ft[:, NB - 1, SLOT2_COL:READY2_COL + 1], ft[:, NB - 1, SLOT_COL:READY_COL + 1]))
                own(dve.tensor_scalar(ft[:, :, LOADED_COL], e_b, 16.0, 48.0, ALU.mult, ALU.add))
                own(dve.tensor_copy(ft[:, :, FIRST_COL], first_b))
                own(dve.tensor_scalar(live, e_b, float(E - 1), None, ALU.is_lt))
                own(dve.tensor_scalar(nblk_b, nblk_b, 1.0, None, ALU.subtract))
                for k in range(3):
                    own(dve.tensor_scalar(fl, nblk_b, float(k), None, ALU.min))
                    own(dve.tensor_tensor(fl, fl, r_b, ALU.is_equal))
                    own(dve.tensor_tensor(ft[:, :, FLAG_COL + k], fl, live, ALU.mult))
                own(dve.tensor_tensor(after, row1(end)[:, E - 1:E].to_broadcast([1, NB]), bidx, ALU.subtract))
                own(dve.tensor_scalar(ft[:, :, MORE_COL], after, 1.5, None, ALU.is_gt))
                own(dve.tensor_scalar(ft[:, :, LAST_COL], after, 1.0, None, ALU.is_equal))
                own(dve.tensor_copy(tab[0:1, 0:NB, 0:LAST_COL + 1], ft[:, :, 0:LAST_COL + 1]))
                dve.tensor_copy(tab[0:1, 0:NB, OTHER_COL:FLAG_COL + 3], ft[:, :, OTHER_COL:FLAG_COL + 3]).then_inc(tables, 1)

            def next_set(c, due, ks):
                for k in ks:
                    with dve.If(due[k] > 0):
                        other, first, loaded, before = table_entries(dve, c, range(OTHER_COL, BEFORE_COL + 1))
                        dve.wait_ge(whi, before + (k + 4))
                        dve.wait_ge(wlo, before + (k + 3))
                        lo, hi = (wbuf[:, ds(other, 1), k, part, :, :].rearrange("p a k c -> p (a k) c") for part in (LO, HI))
                        dve.tensor_tensor(lo, wraw[:, k, :, :], hi.bitcast(F32), ALU.subtract).then_inc(wlo, 1)

            def add_routed(n, b, u, count):
                dve.wait_ge(y_done, n + 1)
                dve.wait_ge(zg_in[u], count)
                dve.scalar_tensor_tensor(out=zg[:, u, :], in0=yb[:, :], scalar=slotinfo[:, 2, ds(b, 1)], in1=zg[:, u, :],
                                         op0=ALU.mult, op1=ALU.add).then_inc(y_used, 1)

            for n in range(NT - RING, NT):
                i = n - (NT - RING)
                if i == 0:
                    choose()
                if i == 1:
                    place()
                if i == 2:
                    slot_tables()
                h_lo(n, n % 2)
                gated(n + 1, (n + 1) % 2)
                if n >= NT - 2:
                    x_lo(n + 2, n % 2)
                add_shared(n)
                if i == 2:
                    block_table()
            def step(b, u, j, base):
                h_lo(b + NT, u % 2)
                gated(b + (NT + 1), 1 - u % 2)
                x_lo(b + (NT + 2), u % 2)
                due = table_entries(dve, b + 1, range(FLAG_COL, FLAG_COL + 3))
                next_set(b + 1, due, (GATE, UP))
                add_routed(b + NT, b, u, j * 16 + 16 * (base + 1))
                next_set(b + 1, due, (DOWN,))

            def last(b, u, j, base):
                h_lo(b + NT, u % 2)
                add_routed(b + NT, b, u, j * 16 + 16 * (base + 1))

            dve.wait_ge(tables, 1)
            next_set(0, table_entries(dve, 0, range(FLAG_COL, FLAG_COL + 3)), range(3))
            groups(dve, step, last)

        @block.tensor
        def _(pe):
            pe.wait_ge(consts, N_CONSTS)
            for b in range(B):
                if b >= 2:
                    pe.wait_ge(chan_done, b - 1)
                aT = GU[:, 2 * (b % 2):2 * (b % 2) + 2, :].rearrange("p a (h t) -> p (a h) t", t=TPB)
                for h in range(2):
                    t = 2 * b + h
                    pe.wait_ge(a_ready, t + 1)
                    for k in range(KC):
                        last = pe.transpose(aT[:, k, h * P:(h + 1) * P], aring[:, t % RING, k * P:(k + 1) * P], ident[:, :])
                last.then_inc(aT_ready, 1)
            ub = scratch[:, 0:NV].rearrange("p (s r) -> p s r", s=KC * 3)
            pe.wait_ge(ub_ready, 1)
            pe.wait_ge(chan_done, B)
            V = GU[:, 0:3, :].rearrange("p a c -> p (a c)")
            for s in range(KC * 3):
                last = pe.transpose(V[:, s * P:(s + 1) * P], ub[:, s, :], ident[:, :])
            last.then_inc(v_ready, 1)
            for i in range(SEARCH_STEPS):
                pe.wait_ge(below, i + 1)
                pe.matmul(yb[:, 0:1], bdiag[:, :, :].rearrange("p b r -> p (b r)"), med[:, 2:3], start=True, stop=True).then_inc(n_below, 1)
            pe.wait_ge(medd_ready, 1)
            pe.matmul(yb[:, 8:8 + B], ones[:, :], medd[:, :], start=True, stop=True).then_inc(med_b, 1)

            def spread_gate(b, u):
                pe.wait_ge(diag_ready, b + 1)
                if not (isinstance(b, int) and b == 0):
                    pe.wait_ge(gate_used, 2 * b if isinstance(b, int) else b * 2)
                pe.matmul(ms[:, :], ones[:, :], diag[:, u, :], start=True, stop=True).then_inc(gate_bc, 1)

            def transpose_x(n, src):
                if not (isinstance(n, int) and n == 0):
                    pe.wait_ge(xlo, n)
                for k in range(KC):
                    last = pe.transpose(tx[:, k * P:(k + 1) * P], src[:, k * P:(k + 1) * P], ident[:, :])
                last.then_inc(tx_done, 1)

            def transpose_h(n, parity):
                pe.wait_ge(hid, n + 1)
                if not (isinstance(n, int) and n == 0):
                    pe.wait_ge(hlo, n)
                for k in range(KC):
                    last = pe.transpose(th[:, k * P:(k + 1) * P], sg[:, parity, k * P:(k + 1) * P], ident[:, :])
                last.then_inc(th_done, 1)

            def product(dst, left, q, k):
                i = 0
                for kc in range(KC):
                    for lp, wp in ((HI, HI), (HI, LO), (LO, HI)):
                        last = pe.matmul(dst, left[:, lp, kc, :], wset(q, k, wp, kc), start=(i == 0), stop=(i == 3 * KC - 1))
                        i += 1
                return last

            def gate_product(n, slot, parity, q, before):
                pe.wait_ge(wlo, before + 1)
                pe.wait_ge(xlo, n + 1)
                product(gu(parity, GATE), xT[:, slot], q, GATE).then_inc(g_done, 1)

            def up_product(n, slot, parity, q, before):
                pe.wait_ge(wlo, before + 2)
                product(gu(parity, UP), xT[:, slot], q, UP).then_inc(u_done, 1)

            def down_product(n, parity, q, before):
                pe.wait_ge(wlo, before + 3)
                pe.wait_ge(hlo, n + 1)
                if not (isinstance(n, int) and n == 0):
                    pe.wait_ge(y_used, n)
                product(yb[:, :], hT[:, parity], q, DOWN).then_inc(y_done, 1)

            def route(t, slot):
                pe.wait_ge(xlo, t + 1)
                if not (isinstance(t, int) and t == 0):
                    pe.wait_ge(logits_used, t)
                for kc in range(KC):
                    for lp in (HI, LO):
                        last = pe.matmul(th[:, 0:2 * E], xT[:, slot, lp, kc, :], rhl[:, kc, :, :].rearrange("p h e -> p (h e)"),
                                         start=(kc == 0 and lp == HI), stop=(kc == KC - 1 and lp == LO))
                last.then_inc(logits, 1)

            pe.wait_ge(rhl_ready, 1)
            spread_gate(0, 0)
            for t in range(RING):
                pe.wait_ge(xn_ready, t + 1)
                if t == 1:
                    spread_gate(1, 1)
                if t == 3:
                    spread_gate(2, 0)
                transpose_x(t, aring[:, t, :])
                route(t, t)
            gate_product(0, 0, 0, 0, 0)
            up_product(0, 0, 0, 0, 0)
            with pe.Fori(0, NT // RING - 1) as j:
                for u in range(RING):
                    n = j * RING + u
                    gate_product(n + 1, (u + 1) % RING, (u + 1) % 2, 0, 0)
                    pe.wait_ge(logits_used, n + RING)
                    transpose_h(n, u % 2)
                    up_product(n + 1, (u + 1) % RING, (u + 1) % 2, 0, 0)
                    pe.wait_ge(xn_ready, n + RING + 1)
                    transpose_x(n + RING, aring[:, u, :])
                    if u % 2 == 1:
                        spread_gate(j * 2 + (3 + u // 2), (3 + u // 2) % 2)
                    down_product(n, u % 2, 0, 0)
                    route(n + RING, u)

            def rank():
                pe.wait_ge(onehot_ready, 1)
                oh = rtmp[:, 288:352].bitcast(BF16)
                pe.matmul(ms[:, 0:128], upper[:, :], oh, start=True, stop=False)
                for i in range(NT - 1):
                    pe.matmul(ms[:, (i + 1) * E:NT * E].rearrange("p (t e) -> p t e", e=E), ones_bf[:, :],
                              oh[:, i * E:(i + 1) * E].unsqueeze(1).to_broadcast([P, NT - 1 - i, E]),
                              start=False, stop=(i == NT - 2))
                for i in range(NT):
                    last = pe.matmul(ms[:, 128:136], ones_bf[:, :], oh[:, i * E:(i + 1) * E], start=(i == 0), stop=(i == NT - 1))
                last.then_inc(rank_done, 1)

            def fill_slots():
                nf = 6
                inblk = scratch[:, 0:NT * P // 2].bitcast(BF16).rearrange("p (t s) -> p t s", s=P)
                sel = scratch[:, 1024:1024 + NT * nf * NB // 2].bitcast(BF16).rearrange("p (t n) -> p t n", t=NT)
                pe.wait_ge(sel_ready, 1 + nf)
                for i in range(NT):
                    last = pe.matmul(ms[:, 136:136 + nf * NB], inblk[:, i, :], sel[:, i, :], start=(i == 0), stop=(i == NT - 1))
                last.then_inc(slots_done, 1)

            for n in range(NT - RING, NT):
                q, before = (0, 0) if n + 1 < NT else (1, 3)
                slot = (n + 1) % RING if n + 1 < NT else 0
                gate_product(n + 1, slot, (n + 1) % 2, q, before)
                pe.wait_ge(logits_used, NT)
                transpose_h(n, n % 2)
                up_product(n + 1, slot, (n + 1) % 2, q, before)
                if n == NT - RING:
                    rank()
                if n == NT - RING + 1:
                    fill_slots()
                if n >= NT - 2:
                    pe.wait_ge(xg_in[n + 2 - NT], 16)
                    transpose_x(n + 2, xg[:, n + 2 - NT, :])
                down_product(n, n % 2, 0, 0)

            def step(b, u, j, base):
                n = b + NT
                ahead = (u + 2) % RING
                q, ready, q_after, ready_after = table_entries(pe, b, range(SLOT_COL, READY2_COL + 1))
                gate_product(n + 1, 1 - u % 2, 1 - u % 2, q_after, ready_after)
                transpose_h(n, u % 2)
                up_product(n + 1, 1 - u % 2, 1 - u % 2, q_after, ready_after)
                pe.wait_ge(xg_in[ahead], j * 16 + 16 * (base + 1 + (u + 2) // RING))
                transpose_x(n + 2, xg[:, ahead, :])
                down_product(n, u % 2, q, ready)

            def last(b, u, j, base):
                q, ready = table_entries(pe, b, range(SLOT_COL, READY_COL + 1))
                transpose_h(b + NT, u % 2)
                down_product(b + NT, u % 2, q, ready)

            pe.wait_ge(tables, 1)
            groups(pe, step, last)


def kernel(x, L0_conv_cfc_w, L0_conv_bn_w, L0_conv_bn_b, L0_ffn_router_w, L0_ffn_w1, L0_ffn_v1, L0_ffn_w2,
           L0_ffn_shared_gate, L0_ffn_shared_up, L0_ffn_shared_down):
    import numpy as np
    import concourse.bacc as bacc
    from concourse.bass_utils import run_bass_kernel_spmd

    x = np.asarray(x)
    batch, chans, height, width = x.shape
    kc = chans // P

    def chunks(a):
        a = np.asarray(a).reshape(kc, P, -1)
        return np.ascontiguousarray(a.transpose(1, 0, 2)).reshape(P, -1)

    x_tok = np.ascontiguousarray(x.transpose(0, 2, 3, 1)).reshape(-1, chans)
    cfc = np.asarray(L0_conv_cfc_w)[:, [0, 2, 1]]
    conv_par = np.concatenate([chunks(cfc), chunks(L0_conv_bn_w), chunks(L0_conv_bn_b)], axis=1)
    router = chunks(np.asarray(L0_ffn_router_w).T)
    shared = [np.asarray(a).T for a in (L0_ffn_shared_gate, L0_ffn_shared_up, L0_ffn_shared_down)]
    sets = [shared] + [[np.asarray(a)[e] for a in (L0_ffn_w1, L0_ffn_v1, L0_ffn_w2)] for e in range(len(L0_ffn_w1))]
    weights = np.stack([np.stack([chunks(m) for m in one]) for one in sets])

    nc = bacc.Bacc("TRN2", target_bir_lowering=False, num_devices=1)
    arrays = {"x_tok": x_tok, "conv_par": conv_par, "router": router, "weights": weights}
    ins = [nc.dram_tensor(n, a.shape, F32, kind="ExternalInput").ap() for n, a in arrays.items()]
    xn_d = nc.dram_tensor("xn_d", x_tok.shape, F32).ap()
    z_d = nc.dram_tensor("z_d", x_tok.shape, F32).ap()
    out = nc.dram_tensor("out", x_tok.shape, F32, kind="ExternalOutput").ap()
    program(nc, *ins, xn_d, z_d, out)
    r = run_bass_kernel_spmd(nc, [arrays], core_ids=[0])
    got = r.results[0]["out"]
    return np.ascontiguousarray(got.reshape(batch, height, width, chans).transpose(0, 3, 1, 2))
```

```python
from contextlib import ExitStack

import concourse.bass as bass
from concourse import mybir

F32 = mybir.dt.float32
F32R = mybir.dt.float32r
BF16 = mybir.dt.bfloat16
I32 = mybir.dt.int32
U32 = mybir.dt.uint32
ALU = mybir.AluOpType
ACT = mybir.ActivationFunctionType
AX_X = mybir.AxisListType.X
ds = bass.ds

P = 128
LN_C_EPS = 1e-6
LN_T_EPS = 1e-5
BN_EPS = 1e-5
BIG = 2.0 ** 100
MEAN, STD, MAX = range(3)
GATE, UP, DOWN = range(3)
HI, LO = range(2)
RING = 4
SEARCH_FROM, SEARCH_TO = -24.0, 24.0
SEARCH_STEPS = 7
N_CONSTS = 13
FIELDS = 6
SLOT_COL, READY_COL, SLOT2_COL, READY2_COL = range(4)
TOTAL_COL = 4
OTHER_COL, FIRST_COL, LOADED_COL, BEFORE_COL = range(8, 12)
FLAG_COL, COLS = 12, 16


def program(nc, B, x_tok, conv_par, router, weights, xn_d, z_d, out):
    T, C = x_tok.shape
    TPB = T // B
    NT = T // P
    KC = C // P
    E = router.shape[1] // KC
    NSETS = weights.shape[0]
    NB = -(-(NT + E - 1) // RING) * RING
    NV = 3 * C
    TPART = P // B
    SURE = (NT - 1) // RING * RING
    assert C == 512 and KC == 4 and TPB == 2 * P and NSETS == E + 1 and E == 8

    with ExitStack() as ctx:
        def sb(name, shape, dt=F32):
            return ctx.enter_context(nc.sbuf_tensor(name, shape, dt))

        def ps(name, shape, dt=F32):
            return ctx.enter_context(nc.psum_tensor(name, shape, dt))

        def sem(name):
            return ctx.enter_context(nc.semaphore(name))

        x_sb = sb("x_sb", [P, NT, C])
        w_parts = sb("w_parts", [P, 2, 3, 2, KC, C], F32R)
        w_raw = sb("w_raw", [P, 3, KC, C])
        xT = sb("xT", [P, RING, 2, KC, P], F32R)
        tiles = sb("tiles", [P, RING, C])
        hidden = sb("hidden", [P, 2, C])
        hT = sb("hT", [P, 2, 2, KC, P], F32R)
        diag = sb("diag", [P, 2, C], F32R)
        scratch = sb("scratch", [P, 2176])
        xg = tiles
        zg = x_sb[:, 0:RING, :]
        ident = sb("ident", [P, P])
        ones = sb("ones", [P, P])
        ones_r = sb("ones_r", [P, P], F32R)
        ones_bf = sb("ones_bf", [P, P], BF16)
        upper = sb("upper", [P, P], BF16)
        same_batch = sb("same_batch", [P, B, TPART])
        batch_pick = sb("batch_pick", [P, B])
        iota_f = sb("iota_f", [P, P])
        iota_i = scratch[:, 0:P].bitcast(I32)
        pidx_i = sb("pidx_i", [P, 2], I32)
        pidx = sb("pidx", [P, 2])
        tile_start = sb("tile_start", [P, NT])
        rev8 = sb("rev8", [P, E])
        powers = sb("powers", [P, 4, B * KC])
        eps = sb("eps", [P, 1])
        room = sb("room", [P, 1])
        steps = sb("steps", [P, 2, SEARCH_STEPS])
        conv = sb("conv", [P, KC * 5])
        router_w = sb("router_w", [P, KC, E])
        router_parts = sb("router_parts", [P, KC, 2, E], F32R)
        bn_parts = sb("bn_parts", [P, 4, 6])
        tok_mv = sb("tok_mv", [P, NT, 2])
        tok_rstd = sb("tok_rstd", [P, NT])
        tok_shift = sb("tok_shift", [P, NT])
        x1_mv = sb("x1_mv", [P, RING, 2])
        x1_rstd = sb("x1_rstd", [P, RING])
        neg_mean = sb("neg_mean", [P, B, KC // 2])
        stats = sb("stats", [P, B, KC, 3])
        count_junk = xT[:, :, :, :, :].rearrange("p r i k t -> p (r i k t)")[:, 0:NV]
        stats_tmp = tiles[:, 3, 0:B * KC * 3].rearrange("p (b s) -> p b s", b=B)
        z = sb("z", [P, B, KC])
        gates_hi = sb("gates_hi", [P, B + 1, KC], F32R)
        gates = sb("gates", [P, B + 1, KC])
        search = sb("search", [P, 16])
        sign_sum = sb("sign_sum", [P, 2])
        med_diag = sb("med_diag", [P, B])
        warm = sb("warm", [P, 2])
        logit_parts = sb("logit_parts", [P, NT, 2 * E])
        route_w = sb("route_w", [P, NT])
        slotinfo = sb("slotinfo", [P, 3, NB])
        tokidx = sb("tokidx", [P, NB], U32)
        scatidx = sb("scatidx", [P, NB], U32)
        rtmp = tiles[:, :, :].rearrange("p a c -> p (a c)")
        tab = scratch[0:1, 1024:1024 + (NB + 1) * COLS].bitcast(I32).rearrange("p (b c) -> p b c", c=COLS)

        GU = ps("GU", [P, 4, C])
        th = ps("th", [P, C])
        tx = ps("tx", [P, C])
        yb = ps("yb", [P, C])
        mb = ps("mb", [P, C])

        x_in = [sem(f"x_in{b}") for b in range(B)]
        conv_in = sem("conv_in")
        router_in = sem("router_in")
        w_in = [sem(f"w_in{k}") for k in range(3)]
        whi = sem("whi")
        wlo = sem("wlo")
        dve_own = sem("dve_own")
        pool_own = sem("pool_own")
        iotas = sem("iotas")
        consts = sem("consts")
        stats_a = sem("stats_a")
        rstd_a = sem("rstd_a")
        a_ready = sem("a_ready")
        aT_ready = sem("aT_ready")
        bank_measured = sem("bank_measured")
        means = sem("means")
        squares = sem("squares")
        std_done = sem("std_done")
        spread_ready = sem("spread_ready")
        v_ready = sem("v_ready")
        thr_ready = sem("thr_ready")
        pen_ready = sem("pen_ready")
        v1_counted = sem("v1_counted")
        sign_summed = sem("sign_summed")
        signs = sem("signs")
        below = sem("below")
        n_below = sem("n_below")
        med_diag_ready = sem("med_diag_ready")
        medians_ready = sem("medians_ready")
        z_ready = sem("z_ready")
        g_ready = sem("g_ready")
        diag_ready = sem("diag_ready")
        gates_spread = sem("gates_spread")
        gate_used = sem("gate_used")
        warmed = sem("warmed")
        a_again = sem("a_again")
        x1_ready = sem("x1_ready")
        x1_measured = sem("x1_measured")
        x1_eps = sem("x1_eps")
        stats_b = sem("stats_b")
        rstd_b = sem("rstd_b")
        xn_ready = sem("xn_ready")
        xn_out = [sem(f"xn_out{u}") for u in range(RING)]
        tx_done = sem("tx_done")
        xhi = sem("xhi")
        xlo = sem("xlo")
        g_done = sem("g_done")
        u_done = sem("u_done")
        silu = sem("silu")
        hid_ready = sem("hid_ready")
        th_done = sem("th_done")
        hhi = sem("hhi")
        hlo = sem("hlo")
        y_done = sem("y_done")
        y_used = sem("y_used")
        z_out = sem("z_out")
        xg_in = [sem(f"xg_in{u}") for u in range(RING)]
        zg_in = [sem(f"zg_in{u}") for u in range(RING)]
        o_out = [sem(f"o_out{u}") for u in range(RING)]
        router_ready = sem("router_ready")
        logits = sem("logits")
        logits_used = sem("logits_used")
        chosen_ready = sem("chosen_ready")
        w_ready = sem("w_ready")
        rank_done = sem("rank_done")
        sel_ready = sem("sel_ready")
        slots_done = sem("slots_done")
        slots_ready = sem("slots_ready")
        tables = sem("tables")

        RANKS, COUNTS = slice(0, NT * E), slice(NT * E, NT * E + E)
        SLOTS = slice(COUNTS.stop, COUNTS.stop + FIELDS * NB)

        block = ctx.enter_context(nc.Block())


        def gu(parity, which):
            return GU[:, 2 * parity + which, :]

        def wset(q, k, part, kc):
            if isinstance(q, int):
                return w_parts[:, q, k, part, kc, :]
            return w_parts[:, ds(q, 1), k, part, kc, :].rearrange("p a c -> p (a c)")

        def tile_of(buf, t):
            if isinstance(t, int):
                return buf[:, t, :]
            return buf[:, ds(t, 1), :].rearrange("p a c -> p (a c)")

        def chosen_flat():
            at = 2 * NT * E + 2 * NT
            return rtmp[:, at:at + NT * E // 2].bitcast(BF16)

        def slot_matrices():
            inblk = scratch[:, 0:NT * P // 2].bitcast(BF16).rearrange("p (t s) -> p t s", s=P)
            sel = scratch[:, NT * P // 2:NT * (P + FIELDS * NB) // 2].bitcast(BF16)
            return inblk, sel.rearrange("p (t n) -> p t n", t=NT)

        def table_entries(eng, c, cols):
            lowest = {READY_COL: 3, READY2_COL: 3, BEFORE_COL: 3, LOADED_COL: 48, TOTAL_COL: NT}
            highest = {READY_COL: 3 * NSETS, READY2_COL: 3 * NSETS, BEFORE_COL: 3 * NSETS, LOADED_COL: 16 * (NSETS + 1),
                       FIRST_COL: NB, TOTAL_COL: NB}
            at = slice(c, c + 1) if isinstance(c, int) else ds(c, 1)
            row = tab[0:1, at, cols.start:cols.stop]
            _, got = nc.values_load_multi_w_load_instructions(row.rearrange("p b c -> p (b c)"), engines=[eng.engine])
            return [nc.s_assert_within(v, lowest.get(col, 0), highest.get(col, 1))
                    for v, col in zip(got, cols)]

        def needed_blocks(eng):
            return table_entries(eng, 0, range(TOTAL_COL, TOTAL_COL + 1))[0]

        def groups(eng, step, last):
            needed = needed_blocks(eng)
            with eng.Fori(0, SURE // RING) as j:
                for u in range(RING):
                    step(j * RING + u, u, j, 0)
            with eng.Fori(0, (NB - SURE) // RING) as j:
                for u in range(RING):
                    b = j * RING + (SURE + u)
                    with eng.If(needed > b + 1):
                        step(b, u, j, SURE // RING)
                    with eng.If(needed == b + 1):
                        last(b, u, j, SURE // RING)

        @block.sync
        def _(sp):
            def load_w(q, k):
                src = weights[q, k] if isinstance(q, int) else weights[ds(q, 1), k, :, :].rearrange("a p n -> (a p) n")
                sp.dma_start(w_raw[:, k, :, :].rearrange("p k c -> p (k c)"), src).then_inc(w_in[k], 16)

            xv = x_tok.rearrange("(b t p) c -> b p t c", p=P, t=2)
            for b in range(B):
                sp.dma_start(x_sb[:, 2 * b:2 * b + 2, :], xv[b]).then_inc(x_in[b], 16)
            sp.dma_start(conv[:, :], conv_par).then_inc(conv_in, 16)
            sp.dma_start(router_w[:, :, :], router.rearrange("p (k e) -> p k e", k=KC)).then_inc(router_in, 16)
            for k in range(3):
                load_w(0, k)
            for k in range(3):
                sp.wait_ge(wlo, k + 1)
                load_w(1, k)

            def store_xn(t, u):
                sp.wait_ge(xn_ready, t + 1)
                sp.dma_start(xn_d[ds(t * P, P), :], tiles[:, u, :]).then_inc(xn_out[u], 16)

            def store_z(t):
                sp.wait_ge(y_used, t + 1)
                sp.dma_start(z_d[ds(t * P, P), :], tile_of(x_sb, t)).then_inc(z_out, 16)

            for t in range(RING):
                store_xn(t, t)
            with sp.Fori(0, NT // RING - 1) as j:
                for u in range(RING):
                    store_xn(j * RING + (RING + u), u)
                    store_z(j * RING + u)
            for k in range(3):
                if k == DOWN:
                    for t in range(NT - RING, NT - 1):
                        store_z(t)
                sp.wait_ge(wlo, 3 + k + 1)
                load_w(2, k)
            store_z(NT - 1)
            with sp.Fori(3, NSETS) as q:
                for k in range(3):
                    sp.wait_ge(wlo, q * 3 + (k - 2))
                    load_w(q, k)

        @block.gpsimd
        def _(pool):
            n_own = [0]

            def own(ins):
                n_own[0] += 1
                ins.then_inc(pool_own, 1)
                pool.wait_ge(pool_own, n_own[0])

            pool.iota(iota_i[:, :], pattern=[[1, P]], base=0, channel_multiplier=0).then_inc(iotas, 1)
            pool.iota(pidx_i[:, :], pattern=[[0, 2]], base=0, channel_multiplier=1).then_inc(iotas, 1)
            pool.memset(powers[:, 0, :], -0.5).then_inc(consts, 1)
            pool.memset(powers[:, 1, :], 0.5).then_inc(consts, 1)
            pool.memset(powers[:, 2, :], -1.0).then_inc(consts, 1)
            pool.memset(powers[:, 3, :], 2.718281828459045).then_inc(consts, 1)
            pool.memset(eps[:, :], LN_T_EPS).then_inc(consts, 1)
            pool.memset(ones[:, :], 1.0).then_inc(consts, 1)
            pool.memset(room[:, :], NV // 2 - 0.5 - C / 2).then_inc(consts, 1)
            pool.memset(ones_bf[:, :], 1.0).then_inc(consts, 1)
            pool.memset(gates[:, B, :], 0.0).then_inc(consts, 1)
            pool.memset(ident[:, :], 0.0).then_inc(pool_own, 1)
            pool.memset(batch_pick[:, :], 0.0).then_inc(pool_own, 1)
            pool.memset(same_batch[:, :, :], 1.0).then_inc(pool_own, 1)
            n_own[0] = 3
            own(pool.memset(upper[:, :], 1.0))
            pool.affine_select(out=ident[:, :], in_=ident[:, :], compare_op=ALU.not_equal, fill=1.0, base=0,
                               pattern=[[-1, P]], channel_multiplier=1).then_inc(consts, 1)
            pool.affine_select(out=batch_pick[:, :], in_=batch_pick[:, :], compare_op=ALU.not_equal, fill=1.0, base=0,
                               pattern=[[-TPART, B]], channel_multiplier=1).then_inc(consts, 1)
            pool.affine_select(out=upper[:, :], in_=upper[:, :], compare_op=ALU.is_gt, fill=0.0, base=0,
                               pattern=[[1, P]], channel_multiplier=-1).then_inc(consts, 1)
            own(pool.affine_select(out=same_batch[:, :, :], in_=same_batch[:, :, :], compare_op=ALU.is_ge, fill=0.0, base=0,
                                   pattern=[[-TPART, B], [0, TPART]], channel_multiplier=1))
            pool.affine_select(out=same_batch[:, :, :], in_=same_batch[:, :, :], compare_op=ALU.is_ge, fill=0.0,
                               base=TPART - 1, pattern=[[TPART, B], [0, TPART]], channel_multiplier=-1).then_inc(consts, 1)
            pool.wait_ge(consts, N_CONSTS)

            def token_rstd(b):
                pool.wait_ge(stats_a, b + 1)
                r, m = tok_rstd[:, 2 * b:2 * b + 2], tok_shift[:, 2 * b:2 * b + 2]
                pool.tensor_scalar(m, tok_mv[:, 2 * b:2 * b + 2, 0], -1.0, None, ALU.mult).then_inc(pool_own, 1)
                n_own[0] += 1
                own(pool.tensor_scalar(r, tok_mv[:, 2 * b:2 * b + 2, 1], LN_C_EPS, None, ALU.add))
                own(pool.tensor_tensor(r, r, powers[:, 0, 0:2], ALU.pow))
                pool.tensor_tensor(m, m, r, ALU.mult).then_inc(rstd_a, 1)

            def channel_std(b):
                pool.wait_ge(squares, 2 * (b + 1))
                own(pool.tensor_scalar(z[:, b, 2:4], z[:, b, 2:4], 1.0 / (TPB - 1), None, ALU.mult))
                pool.wait_ge(bank_measured, 2 * b + 1)
                own(pool.tensor_scalar(z[:, b, 0:2], stats[:, b, 0:2, STD], float(TPB) / (TPB - 1), None, ALU.mult))
                pool.tensor_tensor(stats[:, b, :, STD], z[:, b, :], powers[:, 1, 0:KC], ALU.pow).then_inc(std_done, 1)

            for b in range(B):
                token_rstd(b)
                if b >= 2:
                    channel_std(b - 2)
            channel_std(B - 2)
            channel_std(B - 1)

            def split_lo(q, k):
                pool.wait_ge(whi, 3 * q + k + 1)
                pool.tensor_tensor(w_parts[:, q % 2, k, LO, :, :], w_raw[:, k, :, :], w_parts[:, q % 2, k, HI, :, :].bitcast(F32),
                                   ALU.subtract).then_inc(wlo, 1)

            for k in range(3):
                split_lo(0, k)

            pool.wait_ge(g_ready, 2)

            def spread_diag(b, part):
                parts = gates_hi[:, :, :].bitcast(F32) if part == HI else gates
                if not (isinstance(b, int) and b == 0):
                    pool.wait_ge(gates_spread, b * 2 + (part - 1))
                src = parts[:, b, :] if isinstance(b, int) else parts[:, ds(b, 1), :].rearrange("p a k -> p (a k)")
                pool.tensor_tensor(diag[:, part, :].rearrange("p (k c) -> p k c", k=KC),
                                   ident[:, :].unsqueeze(1).to_broadcast([P, KC, P]),
                                   src.unsqueeze(2).to_broadcast([P, KC, P]), ALU.mult).then_inc(diag_ready, 1)

            def rstd_tile(t, u):
                pool.wait_ge(stats_b, t + 1)
                r = x1_rstd[:, u:u + 1]
                pool.tensor_tensor(r, x1_mv[:, u, 1:2], eps[:, 0:1], ALU.add).then_inc(x1_eps, 1)
                pool.wait_ge(x1_eps, t + 1)
                pool.tensor_tensor(r, r, powers[:, 0, 0:1], ALU.pow).then_inc(rstd_b, 1)

            spread_diag(0, HI)
            own(pool.tensor_tensor(gates[:, :, :], gates[:, :, :], gates_hi[:, :, :].bitcast(F32), ALU.subtract))
            spread_diag(0, LO)
            spread_diag(1, HI)
            spread_diag(1, LO)
            rstd_tile(0, 0)
            rstd_tile(1, 1)
            spread_diag(2, HI)
            spread_diag(2, LO)
            rstd_tile(2, 2)
            rstd_tile(3, 3)
            with pool.Fori(0, NT // RING - 1) as j:
                for u in range(RING):
                    rstd_tile(j * RING + (RING + u), u)
                    if u % 2 == 1:
                        for part in (HI, LO):
                            spread_diag(j * 2 + (3 + u // 2), part)

            split_lo(1, GATE)
            pool.wait_ge(w_ready, 1)
            own(pool.tensor_tensor(route_w[:, :], powers[:, 3, 0:NT], route_w[:, :], ALU.pow))
            own(pool.tensor_scalar(route_w[:, :], route_w[:, :], 1.0, None, ALU.add))
            pool.tensor_tensor(route_w[:, :], route_w[:, :], powers[:, 2, 0:NT], ALU.pow).then_inc(w_ready, 1)
            split_lo(1, UP)

            def rows(table, b):
                return bass.IndirectOffsetOnAxis(ap=table[:, b:b + 1], axis=0)

            def gather_x(b):
                pool.indirect_dma_start(xg[:, b % RING, :], None, xn_d[:, :], rows(tokidx, b)).then_inc(xg_in[b % RING], 16)

            def gather_z(b):
                pool.indirect_dma_start(zg[:, b % RING, :], None, z_d[:, :], rows(tokidx, b)).then_inc(zg_in[b % RING], 16)

            def scatter(b):
                pool.wait_ge(y_used, NT + b + 1)
                pool.indirect_dma_start(out[:, :], rows(scatidx, b), zg[:, b % RING, :], None,
                                        bounds_check=T - 1, oob_is_err=False).then_inc(o_out[b % RING], 16)

            def stored(b):
                pool.wait_ge(o_out[b % RING], 16 * (b // RING + 1))

            pool.wait_ge(slots_ready, 3)
            for u in range(RING):
                pool.wait_ge(xn_out[u], 16 * (NT // RING))
            pool.wait_ge(tx_done, NT)
            for b in range(RING):
                gather_x(b)
            split_lo(1, DOWN)
            split_lo(2, GATE)
            pool.wait_ge(z_out, 16 * NT)
            for b in range(RING - 1):
                gather_z(b)
            split_lo(2, UP)
            pool.wait_ge(tables, 1)

            def fetch_x(b):
                pool.wait_ge(tx_done, NT + b - RING + 1)
                gather_x(b)

            needed = needed_blocks(pool)
            for b in range(NB):
                c = b + RING - 1
                if c + 1 < NT:
                    fetch_x(c + 1)
                    scatter(b)
                    if b:
                        stored(b - 1)
                    gather_z(c)
                    continue
                if c + 1 < NB:
                    with pool.If(needed > c):
                        fetch_x(c + 1)
                with pool.If(needed > b):
                    scatter(b)
                    stored(b - 1)
                if c < NB:
                    with pool.If(needed > c):
                        gather_z(c)
            for b in range(NT - 1, NB):
                with pool.If(needed == b + 1):
                    stored(b)

        @block.scalar
        def _(act):
            def split_hi(raw, hi):
                act.activation(hi, raw, ACT.Copy).then_inc(whi, 1)

            act.wait_ge(consts, N_CONSTS)
            act.activation(warm[:, 0:1], eps[:, 0:1], ACT.Sigmoid).then_inc(warmed, 1)

            def token_norm(b):
                act.wait_ge(rstd_a, b + 1)
                if b >= 2:
                    act.wait_ge(aT_ready, b - 1)
                for t in (2 * b, 2 * b + 1):
                    act.activation(tiles[:, t % RING, :], x_sb[:, t, :], ACT.Identity, bias=tok_shift[:, t:t + 1],
                                   scale=tok_rstd[:, t:t + 1]).then_inc(a_ready, 1)

            def channel_squares(b):
                aT = GU[:, 2 * (b % 2) + 1, :].rearrange("p (k t) -> p k t", t=TPB)
                junk = scratch[:, P:P + 8 * TPB].rearrange("p (a i k t) -> p a i k t", a=2, i=2, k=2)
                act.wait_ge(aT_ready, b + 1)
                if b >= 2:
                    act.wait_ge(squares, 2 * (b - 1))
                for k in range(2):
                    act.activation(junk[:, b % 2, 0, k, :], aT[:, k, :], ACT.Copy, scale=-1.0 / TPB,
                                   accum_out=neg_mean[:, b, k:k + 1]).then_inc(means, 1)
                act.wait_ge(means, 2 * (b + 1))
                for k in range(2):
                    act.activation(junk[:, b % 2, 1, k, :], aT[:, k, :], ACT.Square, bias=neg_mean[:, b, k:k + 1],
                                   accum_out=z[:, b, 2 + k:3 + k]).then_inc(squares, 1)

            token_norm(0)
            token_norm(1)
            for b in range(B):
                channel_squares(b)
                if b + 2 < B:
                    token_norm(b + 2)

            def first_hi(q, k):
                act.wait_ge(w_in[k], 16 * (q + 1))
                split_hi(w_raw[:, k, :, :], w_parts[:, q, k, HI, :, :])

            for i in range(SEARCH_STEPS):
                act.wait_ge(thr_ready, i + 1)
                act.activation(tiles[:, 3, :], GU[:, 2, :], ACT.Sign, bias=search[:, 3:4], scale=-1.0,
                               accum_out=sign_sum[:, 0:1]).then_inc(sign_summed, 1)
                act.wait_ge(sign_summed, i + 1)
                act.activation(sign_sum[:, 1:2], sign_sum[:, 0:1], ACT.Identity, bias=room[:, 0:1], scale=-0.5).then_inc(signs, 1)
                if i < 3:
                    first_hi(0, i)
            for k in range(2):
                first_hi(1, k)
            act.wait_ge(pen_ready, 2)
            act.activation(count_junk, scratch[:, 0:NV], ACT.Copy, scale=1.0 / BIG, accum_out=search[:, 5:6]).then_inc(v1_counted, 1)
            first_hi(1, DOWN)

            act.wait_ge(z_ready, 1)
            act.activation(gates[:, 0:B, :], z[:, :, :], ACT.Sigmoid, scale=-1.0).then_inc(g_ready, 1)
            act.wait_ge(g_ready, 1)
            act.activation(gates_hi[:, :, :], gates[:, :, :], ACT.Copy).then_inc(g_ready, 1)

            def norm_a(t, u):
                act.wait_ge(z_ready, 1)
                if not isinstance(t, int):
                    act.wait_ge(xn_out[u], (t - u) * 4)
                    act.wait_ge(tx_done, t - 3)
                bias, scale = (v[:, t:t + 1] if isinstance(t, int) else v[:, ds(t, 1)] for v in (tok_shift, tok_rstd))
                act.activation(tiles[:, u, :], tile_of(x_sb, t), ACT.Identity, bias=bias, scale=scale).then_inc(a_again, 1)

            def x_hi(n, slot):
                act.wait_ge(tx_done, n + 1)
                act.activation(xT[:, slot, HI, :, :], tx[:, :].rearrange("p (k t) -> p k t", k=KC), ACT.Copy).then_inc(xhi, 1)

            def silu_gate(n, parity):
                act.wait_ge(g_done, n + 1)
                act.activation(hidden[:, parity, :], gu(parity, GATE), ACT.Silu).then_inc(silu, 1)

            def h_hi(n, parity):
                act.wait_ge(th_done, n + 1)
                act.activation(hT[:, parity, HI, :, :], th[:, :].rearrange("p (k t) -> p k t", k=KC), ACT.Copy).then_inc(hhi, 1)

            norm_a(0, 0)
            norm_a(1, 1)
            norm_a(2, 2)
            norm_a(3, 3)
            act.activation(warm[:, 1:2], eps[:, 0:1], ACT.Silu).then_inc(warmed, 1)
            x_hi(0, 0)
            x_hi(1, 1)
            x_hi(2, 2)
            silu_gate(0, 0)
            x_hi(3, 3)
            with act.Fori(0, NT // RING - 1) as j:
                for u in range(RING):
                    n = j * RING + u
                    norm_a(n + RING, u)
                    h_hi(n, u % 2)
                    silu_gate(n + 1, (u + 1) % 2)
                    x_hi(n + RING, u)
            for n in range(NT - RING, NT - 1):
                h_hi(n, n % 2)
                silu_gate(n + 1, (n + 1) % 2)
            x_hi(NT, 0)
            h_hi(NT - 1, 1)
            silu_gate(NT, 0)
            x_hi(NT + 1, 1)
            for k in (GATE, UP):
                act.wait_ge(w_in[k], 16 * 3)
                act.wait_ge(u_done, NT)
                split_hi(w_raw[:, k, :, :], w_parts[:, 0, k, HI, :, :])

            def next_set(entries):
                other, first, loaded, _, *due = entries
                for k in range(3):
                    with act.If(due[k] > 0):
                        act.wait_ge(w_in[k], loaded)
                        act.wait_ge(y_done if k == DOWN else u_done, first + NT)
                        split_hi(w_raw[:, k, :, :], w_parts[:, ds(other, 1), k, HI, :, :].rearrange("p a k c -> p (a k) c"))

            def step(b, u, j, base):
                h_hi(b + NT, u % 2)
                silu_gate(b + (NT + 1), 1 - u % 2)
                entries = table_entries(act, b + 1, range(OTHER_COL, FLAG_COL + 3))
                x_hi(b + (NT + 2), u % 2)
                next_set(entries)

            def last(b, u, j, base):
                h_hi(b + NT, u % 2)

            act.wait_ge(tables, 1)
            next_set(table_entries(act, 0, range(OTHER_COL, FLAG_COL + 3)))
            groups(act, step, last)

        @block.vector
        def _(dve):
            n_own = [0]

            def note(ins):
                n_own[0] += 1
                ins.then_inc(dve_own, 1)

            def settle():
                dve.wait_ge(dve_own, n_own[0])

            def own(ins):
                note(ins)
                settle()

            dve.wait_ge(iotas, 2)
            dve.tensor_scalar(pidx_i[:, 1:2], pidx_i[:, 1:2], TPART - 1, None, ALU.bitwise_and).then_inc(dve_own, 1)
            n_own[0] += 1
            own(dve.tensor_copy(iota_f[:, :], iota_i[:, :]))
            own(dve.tensor_copy(pidx[:, :], pidx_i[:, :]))
            dve.tensor_scalar(tile_start[:, :], iota_f[:, 0:NT], float(P), None, ALU.mult).then_inc(dve_own, 1)
            dve.tensor_scalar(rev8[:, :], iota_f[:, 0:E], -1.0, float(E), ALU.mult, ALU.add).then_inc(dve_own, 1)
            n_own[0] += 2
            width = SEARCH_TO - SEARCH_FROM
            for i in range(SEARCH_STEPS):
                step = width / (TPART + 1) ** (i + 1)
                dve.memset(steps[:, 0, i:i + 1], step).then_inc(dve_own, 1)
                dve.tensor_scalar(steps[:, 1, i:i + 1], pidx[:, 1:2], 1.0, step, ALU.add, ALU.mult).then_inc(dve_own, 1)
                n_own[0] += 2
            own(dve.memset(search[:, 0:1], SEARCH_FROM))

            def measure(tokens, channels):
                if tokens is not None:
                    dve.wait_ge(x_in[tokens], 16)
                    for h in range(2):
                        note(dve.bn_stats(bn_parts[:, h, :], x_sb[:, 2 * tokens + h, :]))
                if channels is not None:
                    aT = GU[:, 2 * (channels % 2):2 * (channels % 2) + 2, :].rearrange("p a (h t) -> p a h t", t=TPB)
                    dve.wait_ge(aT_ready, channels + 1)
                    for k in range(2):
                        note(dve.bn_stats(bn_parts[:, 2 + k, :], aT[:, 0, k, :]))
                settle()
                if tokens is not None:
                    for h in range(2):
                        note(dve.bn_aggr(tok_mv[:, 2 * tokens + h, :], bn_parts[:, h, :]))
                    dve.engine_nop().then_inc(stats_a, 1)
                if channels is not None:
                    for k in range(2):
                        note(dve.bn_aggr(stats[:, channels, k, 0:2], bn_parts[:, 2 + k, :]))
                    dve.tensor_reduce(stats[:, channels, 0:2, MAX], aT[:, 0, :, :], AX_X, ALU.max).then_inc(bank_measured, 1)
                    dve.wait_ge(squares, 2 * (channels + 1))
                    dve.tensor_reduce(stats[:, channels, 2:4, MAX], aT[:, 1, :, :], AX_X, ALU.max).then_inc(bank_measured, 1)
                settle()

            for b in range(B + 2):
                measure(b if b < B else None, b - 2 if b >= 2 else None)

            dve.wait_ge(consts, N_CONSTS)
            note(dve.tensor_copy(ones_r[:, :], ones[:, :]))
            dve.wait_ge(router_in, 16)
            own(dve.tensor_copy(router_parts[:, :, HI, :], router_w[:, :, :]))
            dve.tensor_tensor(router_parts[:, :, LO, :], router_w[:, :, :], router_parts[:, :, HI, :].bitcast(F32), ALU.subtract).then_inc(router_ready, 1)

            spread_in = scratch[:, 0:NV].rearrange("p (s b r) -> p s b r", s=KC * 3, b=B)
            dve.wait_ge(means, 2 * B)
            own(dve.tensor_scalar(stats[:, :, 2:4, MEAN], neg_mean[:, :, :], -1.0, None, ALU.mult))
            dve.wait_ge(bank_measured, 2 * B)
            dve.wait_ge(std_done, B)
            stats_f = stats[:, :, :, :].rearrange("p b k s -> p b (k s)")
            dve.tensor_copy(spread_in, stats_f.rearrange("p b s -> p s b").unsqueeze(3).to_broadcast([P, KC * 3, B, TPART])).then_inc(spread_ready, 1)
            V = GU[:, 0:3, :].rearrange("p a c -> p (a c)")
            dve.wait_ge(v_ready, 1)
            low, cnt, ind, thr, v1, c1, m2, cand, ahead = (search[:, i:i + 1] for i in range(9))
            junk = tiles[:, 0:3, :].rearrange("p a c -> p (a c)")
            V2 = GU[:, 0:2, :].rearrange("p a c -> p (a c)")
            junk2 = tiles[:, 0:2, :].rearrange("p a c -> p (a c)")
            dve.tensor_tensor(thr, low, steps[:, 1, 0:1], ALU.add).then_inc(thr_ready, 1)
            dve.wait_ge(thr_ready, 1)
            for i in range(SEARCH_STEPS):
                own(dve.tensor_scalar(junk2, V2, thr, 0.0, ALU.is_le, ALU.add, accum_out=cnt))
                if i + 1 < SEARCH_STEPS:
                    note(dve.tensor_tensor(ahead, low, steps[:, 1, i + 1:i + 2], ALU.add))
                dve.wait_ge(signs, i + 1)
                dve.tensor_tensor(ind, cnt, sign_sum[:, 1:2], ALU.is_lt).then_inc(below, 1)
                settle()
                dve.wait_ge(n_below, i + 1)
                if i + 1 < SEARCH_STEPS:
                    dve.scalar_tensor_tensor(out=thr, in0=yb[:, 0:1], scalar=steps[:, 0, i:i + 1], in1=ahead, op0=ALU.mult,
                                             op1=ALU.add).then_inc(thr_ready, 1)
                    dve.wait_ge(thr_ready, i + 2)
                own(dve.scalar_tensor_tensor(out=low, in0=yb[:, 0:1], scalar=steps[:, 0, i:i + 1], in1=low, op0=ALU.mult, op1=ALU.add))

            pen = scratch[:, 0:NV]

            def least(outside, bound, least):
                dve.tensor_scalar(pen, V, bound, BIG, outside, ALU.mult).then_inc(pen_ready, 1)
                dve.wait_ge(pen_ready, 1 if bound is low else 2)
                own(dve.tensor_tensor_reduce(junk, V, pen, 1.0, 3e38, ALU.add, ALU.min, least))

            least(ALU.is_lt, low, v1)
            least(ALU.is_le, v1, m2)
            dve.wait_ge(v1_counted, 1)
            own(dve.tensor_scalar(cand, c1, NV // 2 + 0.5, BIG, ALU.is_lt, ALU.mult))
            own(dve.tensor_tensor(cand, cand, v1, ALU.add))
            own(dve.tensor_tensor(m2, m2, cand, ALU.min))
            own(dve.tensor_tensor(m2, m2, v1, ALU.add))
            dve.tensor_scalar(med_diag[:, :], batch_pick[:, :], m2, 0.5, ALU.mult, ALU.mult).then_inc(med_diag_ready, 1)

            dve.wait_ge(medians_ready, 1)
            cw = conv[:, 0:KC * 3].unsqueeze(1).to_broadcast([P, B, KC * 3])
            own(dve.tensor_tensor(stats_tmp[:, :, :], stats_f, yb[:, 8:8 + B].unsqueeze(2).to_broadcast([P, B, KC * 3]), ALU.subtract))
            own(dve.tensor_tensor(stats_f, stats_tmp[:, :, :], stats_tmp[:, :, :], ALU.mult))
            own(dve.tensor_tensor(stats_f, stats_f, stats_tmp[:, :, :], ALU.mult))
            dve.wait_ge(conv_in, 16)
            own(dve.tensor_tensor(stats_tmp[:, :, :], stats_f, cw, ALU.mult))
            own(dve.tensor_reduce(z[:, :, :], stats_tmp[:, :, :].rearrange("p b (k s) -> p b k s", s=3), AX_X, ALU.add))
            bnw = conv[:, 3 * KC:4 * KC].unsqueeze(1).to_broadcast([P, B, KC])
            bnb = conv[:, 4 * KC:5 * KC].unsqueeze(1).to_broadcast([P, B, KC])
            own(dve.scalar_tensor_tensor(out=z[:, :, :], in0=z[:, :, :], scalar=-1.0 / (1.0 + BN_EPS) ** 0.5, in1=bnw, op0=ALU.mult, op1=ALU.mult))
            dve.tensor_tensor(z[:, :, :], z[:, :, :], bnb, ALU.subtract).then_inc(z_ready, 1)

            def gate_tile(t, u, batch):
                buf, xt = tiles[:, u, :], tile_of(x_sb, t)
                dve.wait_ge(a_again, t + 1)
                dve.wait_ge(gates_spread, batch * 2 + 2)
                dve.tensor_tensor(buf, buf, mb[:, :], ALU.mult).then_inc(gate_used, 1)
                dve.wait_ge(gate_used, t + 1)
                dve.tensor_tensor(xt, xt, buf, ALU.add).then_inc(x1_ready, 1)
                dve.wait_ge(z_ready, 1)
                dve.wait_ge(x1_ready, t + 1)
                dve.bn_stats(bn_parts[:, u, :], xt).then_inc(x1_measured, 1)
                dve.wait_ge(z_ready, 1)
                dve.wait_ge(x1_measured, t + 1)
                dve.bn_aggr(x1_mv[:, u, :], bn_parts[:, u, :]).then_inc(stats_b, 1)

            def norm_tile(t, u):
                dve.wait_ge(rstd_b, t + 1)
                dve.tensor_scalar(tiles[:, u, :], tile_of(x_sb, t), x1_mv[:, u, 0:1], x1_rstd[:, u:u + 1], ALU.subtract, ALU.mult).then_inc(xn_ready, 1)

            def x_lo(n, slot):
                dve.wait_ge(xhi, n + 1)
                dve.tensor_tensor(xT[:, slot, LO, :, :], tx[:, :].rearrange("p (k t) -> p k t", k=KC),
                                  xT[:, slot, HI, :, :].bitcast(F32), ALU.subtract).then_inc(xlo, 1)

            def keep_logits(t, u):
                dve.wait_ge(logits, t + 1)
                dve.tensor_copy(logit_parts[:, t, :] if isinstance(t, int) else tile_of(logit_parts, t), th[:, 0:2 * E]).then_inc(logits_used, 1)

            def h_lo(n, parity):
                dve.wait_ge(hhi, n + 1)
                dve.tensor_tensor(hT[:, parity, LO, :, :], th[:, :].rearrange("p (k t) -> p k t", k=KC),
                                  hT[:, parity, HI, :, :].bitcast(F32), ALU.subtract).then_inc(hlo, 1)

            def gated(n, parity):
                dve.wait_ge(silu, n + 1)
                dve.wait_ge(u_done, n + 1)
                dve.tensor_tensor(hidden[:, parity, :], hidden[:, parity, :], gu(parity, UP), ALU.mult).then_inc(hid_ready, 1)

            def add_shared(t):
                dve.wait_ge(y_done, t + 1)
                xt = tile_of(x_sb, t)
                dve.tensor_tensor(xt, xt, yb[:, :], ALU.add).then_inc(y_used, 1)

            gate_tile(0, 0, 0)
            gate_tile(1, 1, 0)
            norm_tile(0, 0)
            norm_tile(1, 1)
            gate_tile(2, 2, 1)
            x_lo(0, 0)
            gate_tile(3, 3, 1)
            norm_tile(2, 2)
            x_lo(1, 1)
            norm_tile(3, 3)
            x_lo(2, 2)
            keep_logits(0, 0)
            keep_logits(1, 1)
            x_lo(3, 3)
            gated(0, 0)
            keep_logits(2, 2)
            keep_logits(3, 3)
            with dve.Fori(0, NT // RING - 1) as j:
                for u in range(RING):
                    n = j * RING + u
                    t = n + RING
                    gate_tile(t, u, j * 2 + (2 + u // 2))
                    norm_tile(t, u)
                    h_lo(n, u % 2)
                    gated(n + 1, (u + 1) % 2)
                    x_lo(t, u)
                    add_shared(n)
                    keep_logits(t, u)

            def carve(space, at, *widths):
                cuts = [at + sum(widths[:i]) for i in range(len(widths) + 1)]
                return [space[:, i:j] for i, j in zip(cuts, cuts[1:])]

            def by_tile(v):
                return v.rearrange("p (t e) -> p t e", e=E)

            TE = NT * E
            L, score, mx, best, chosen, rank, first_slot, cmp, slot, slot_i, slot_bj, field, wrest, blk = carve(
                rtmp, 0, TE, TE, NT, NT, TE // 2, TE, E, TE, NT, 2 * NT, 2 * NT, NT * FIELDS // 2, NT, NT * NB // 2)
            nblk, end, first = carve(stats[:, :, :, :].rearrange("p b k s -> p (b k s)"), 0, E, E, E)
            L, score, rank, chosen = (by_tile(v) for v in (L, score, rank, chosen.bitcast(BF16)))
            cmp = cmp.rearrange("p (e t) -> p e t", e=E)
            slot_i, slot_bj = (v.rearrange("p (a t) -> p a t", a=2) for v in (slot_i.bitcast(I32), slot_bj))
            field = field.bitcast(BF16).rearrange("p (t f) -> p t f", f=FIELDS)
            blk = blk.bitcast(BF16).rearrange("p (t b) -> p t b", b=NB)
            inblk, sel = slot_matrices()
            sel = sel.rearrange("p t (f b) -> p t f b", f=FIELDS)
            inT = [P, NT, E]

            def choose():
                dve.wait_ge(logits_used, NT)
                for u in range(RING):
                    dve.wait_ge(xn_out[u], 16 * (NT // RING))
                own(dve.tensor_tensor(L, logit_parts[:, :, 0:E], logit_parts[:, :, E:2 * E], ALU.add))
                own(dve.tensor_reduce(mx, L, AX_X, ALU.max))
                dve.tensor_scalar(route_w[:, :], mx, -1.0, None, ALU.mult).then_inc(w_ready, 1)
                own(dve.tensor_tensor(score, L, mx.unsqueeze(2).to_broadcast(inT), ALU.is_equal))
                rev = rev8[:, :].unsqueeze(1).to_broadcast(inT)
                own(dve.tensor_tensor(score, score, rev, ALU.mult))
                own(dve.tensor_reduce(best, score, AX_X, ALU.max))
                dve.tensor_tensor(chosen, best.unsqueeze(2).to_broadcast(inT), rev, ALU.is_equal).then_inc(chosen_ready, 1)

            def place():
                dve.wait_ge(rank_done, 1)
                counts = mb[:, COUNTS].unsqueeze(2).to_broadcast([P, E, NT])
                own(dve.tensor_tensor(cmp, tile_start[:, :].unsqueeze(1).to_broadcast([P, E, NT]), counts, ALU.is_lt))
                own(dve.tensor_reduce(nblk, cmp, AX_X, ALU.add))
                own(dve.tensor_scalar(nblk, nblk, 1.0, None, ALU.max))
                own(dve.tensor_tensor_scan(end, ones[:, 0:E], nblk, 0.0, ALU.mult, ALU.add))
                own(dve.tensor_tensor(first, end, nblk, ALU.subtract))
                own(dve.tensor_scalar(first_slot, first, float(P), None, ALU.mult))
                own(dve.tensor_tensor(rank, by_tile(mb[:, RANKS]), first_slot.unsqueeze(1).to_broadcast(inT), ALU.add))
                own(dve.tensor_tensor(rank, rank, chosen, ALU.mult))
                own(dve.tensor_reduce(slot, rank, AX_X, ALU.add))
                own(dve.tensor_copy(slot_i[:, 0, :], slot))
                own(dve.tensor_scalar(slot_i[:, 1, :], slot_i[:, 0, :], P - 1, None, ALU.bitwise_and))
                own(dve.tensor_scalar(slot_i[:, 0, :], slot_i[:, 0, :], P.bit_length() - 1, None, ALU.logical_shift_right))
                own(dve.tensor_copy(slot_bj, slot_i))
                dve.tensor_tensor(inblk, iota_f[:, :].unsqueeze(1).to_broadcast([P, NT, P]),
                                  slot_bj[:, 1, :].unsqueeze(2).to_broadcast([P, NT, P]), ALU.is_equal).then_inc(sel_ready, 1)
                own(dve.tensor_tensor(blk, iota_f[:, 0:NB].unsqueeze(1).to_broadcast([P, NT, NB]),
                                      slot_bj[:, 0, :].unsqueeze(2).to_broadcast([P, NT, NB]), ALU.is_equal))

            def fields():
                dve.wait_ge(w_ready, 2)
                own(dve.tensor_copy(field[:, :, 0], pidx[:, 0:1].to_broadcast([P, NT])))
                own(dve.tensor_copy(field[:, :, 1], tile_start[:, :]))
                own(dve.memset(field[:, :, 2], 1.0))
                own(dve.tensor_copy(field[:, :, 3], route_w[:, :]))
                own(dve.tensor_tensor(wrest, route_w[:, :], field[:, :, 3], ALU.subtract))
                own(dve.tensor_copy(field[:, :, 4], wrest))
                own(dve.tensor_tensor(wrest, wrest, field[:, :, 4], ALU.subtract))
                own(dve.tensor_copy(field[:, :, 5], wrest))
                for f in range(FIELDS):
                    dve.tensor_tensor(sel[:, :, f, :], blk, field[:, :, f].unsqueeze(2).to_broadcast([P, NT, NB]),
                                      ALU.mult).then_inc(sel_ready, 1)

            def slot_tables():
                dve.wait_ge(slots_done, 1)
                S = mb[:, SLOTS].rearrange("p (f b) -> p f b", f=FIELDS)
                tok, row, wgt = (slotinfo[:, i, :] for i in range(3))
                own(dve.tensor_copy(tok, S[:, 0, :]))
                own(dve.tensor_tensor(tok, tok, S[:, 1, :], ALU.add))
                dve.tensor_copy(tokidx[:, :], tok).then_inc(slots_ready, 1)
                own(dve.tensor_scalar(row, S[:, 2, :], -2.0 * T, 2.0 * T, ALU.mult, ALU.add))
                own(dve.tensor_tensor(row, row, tok, ALU.add))
                dve.tensor_copy(scatidx[:, :], row).then_inc(slots_ready, 1)
                own(dve.tensor_copy(wgt, S[:, 5, :]))
                own(dve.tensor_tensor(wgt, wgt, S[:, 4, :], ALU.add))
                dve.tensor_tensor(wgt, wgt, S[:, 3, :], ALU.add).then_inc(slots_ready, 1)

            be = [1, NB, E]
            ft, c3, oh, e_b, first_b, nblk_b, r_b, fl, live, ei = carve(scratch[0:1, :], 0, NB * COLS, NB * E, NB * E, *[NB] * 7)
            ft = ft.rearrange("p (b c) -> p b c", c=COLS)
            c3, oh = (v.rearrange("p (b e) -> p b e", e=E) for v in (c3, oh))
            ei = ei.bitcast(I32)
            bidx = iota_f[0:1, 0:NB]
            n_e, end_e, first_e = (v[0:1, :] for v in (nblk, end, first))

            def block_experts():
                own(dve.tensor_tensor(c3, end_e.unsqueeze(1).to_broadcast(be), bidx.unsqueeze(2).to_broadcast(be), ALU.is_le))
                own(dve.tensor_reduce(e_b, c3, AX_X, ALU.add))
                own(dve.tensor_scalar(e_b, e_b, float(E - 1), None, ALU.min))
                own(dve.tensor_tensor(oh, iota_f[0:1, 0:E].unsqueeze(1).to_broadcast(be), e_b.unsqueeze(2).to_broadcast(be), ALU.is_equal))
                own(dve.tensor_tensor(c3, oh, first_e.unsqueeze(1).to_broadcast(be), ALU.mult))
                own(dve.tensor_reduce(first_b, c3, AX_X, ALU.add))
                own(dve.tensor_tensor(c3, oh, n_e.unsqueeze(1).to_broadcast(be), ALU.mult))
                own(dve.tensor_reduce(nblk_b, c3, AX_X, ALU.add))

            def block_table():
                note(dve.tensor_tensor(r_b, bidx, first_b, ALU.subtract))
                note(dve.tensor_copy(ei, e_b))
                note(dve.tensor_scalar(live, e_b, float(E - 1), None, ALU.is_lt))
                note(dve.tensor_scalar(fl, nblk_b, 2.0, -1.0, ALU.min, ALU.add))
                note(dve.tensor_scalar(ft[:, :, READY_COL], e_b, 3.0, 3.0, ALU.mult, ALU.add))
                note(dve.tensor_scalar(ft[:, :, BEFORE_COL], e_b, 3.0, 3.0, ALU.mult, ALU.add))
                note(dve.tensor_scalar(ft[:, :, LOADED_COL], e_b, 16.0, 48.0, ALU.mult, ALU.add))
                note(dve.tensor_copy(ft[:, :, FIRST_COL], first_b))
                note(dve.tensor_copy(ft[:, :, TOTAL_COL], end_e[:, E - 1:E].to_broadcast([1, NB])))
                settle()
                note(dve.scalar_tensor_tensor(out=ft[:, :, FLAG_COL + GATE], in0=r_b, scalar=0.0, in1=live, op0=ALU.is_equal, op1=ALU.mult))
                note(dve.scalar_tensor_tensor(out=ft[:, :, FLAG_COL + UP], in0=r_b, scalar=0.0, in1=live, op0=ALU.is_equal, op1=ALU.mult))
                note(dve.tensor_tensor(fl, fl, r_b, ALU.is_equal))
                own(dve.tensor_scalar(ei, ei, 1, None, ALU.bitwise_and))
                note(dve.memset(ft[:, 0, FLAG_COL:FLAG_COL + 2], 0.0))
                note(dve.tensor_tensor(ft[:, :, FLAG_COL + DOWN], fl, live, ALU.mult))
                own(dve.tensor_copy(ft[:, :, OTHER_COL], ei))
                own(dve.tensor_scalar(ft[:, :, SLOT_COL], ft[:, :, OTHER_COL], -1.0, 1.0, ALU.mult, ALU.add))
                note(dve.tensor_copy(ft[:, 0:NB - 1, SLOT2_COL:READY2_COL + 1], ft[:, 1:NB, SLOT_COL:READY_COL + 1]))
                own(dve.tensor_copy(ft[:, NB - 1, SLOT2_COL:READY2_COL + 1], ft[:, NB - 1, SLOT_COL:READY_COL + 1]))
                note(dve.tensor_copy(tab[0:1, 0:NB, 0:TOTAL_COL + 1], ft[:, :, 0:TOTAL_COL + 1]))
                own(dve.tensor_copy(tab[0:1, 0:NB, OTHER_COL:FLAG_COL + 3], ft[:, :, OTHER_COL:FLAG_COL + 3]))
                dve.engine_nop().then_inc(tables, 1)

            def next_set(entries, ks):
                other, _, _, before, *due = entries
                for k in ks:
                    with dve.If(due[k] > 0):
                        dve.wait_ge(whi, before + (k + 4))
                        dve.wait_ge(wlo, before + (k + 3))
                        lo, hi = (w_parts[:, ds(other, 1), k, part, :, :].rearrange("p a k c -> p (a k) c") for part in (LO, HI))
                        dve.tensor_tensor(lo, w_raw[:, k, :, :], hi.bitcast(F32), ALU.subtract).then_inc(wlo, 1)

            def add_routed(n, b, u, count):
                dve.wait_ge(y_done, n + 1)
                dve.wait_ge(zg_in[u], count)
                dve.scalar_tensor_tensor(out=zg[:, u, :], in0=yb[:, :], scalar=slotinfo[:, 2, ds(b, 1)], in1=zg[:, u, :],
                                         op0=ALU.mult, op1=ALU.add).then_inc(y_used, 1)

            n = NT - RING
            choose()
            h_lo(n, 0)
            gated(n + 1, 1)
            place()
            add_shared(n)
            h_lo(n + 1, 1)
            gated(n + 2, 0)
            fields()
            add_shared(n + 1)
            slot_tables()
            h_lo(n + 2, 0)
            gated(n + 3, 1)
            block_experts()
            x_lo(n + 4, 0)
            add_shared(n + 2)
            h_lo(n + 3, 1)
            block_table()
            add_shared(n + 3)
            x_lo(n + 5, 1)
            gated(n + 4, 0)

            def step(b, u, j, base):
                h_lo(b + NT, u % 2)
                entries = table_entries(dve, b + 1, range(OTHER_COL, FLAG_COL + 3))
                gated(b + (NT + 1), 1 - u % 2)
                x_lo(b + (NT + 2), u % 2)
                next_set(entries, (GATE, UP))
                add_routed(b + NT, b, u, j * 16 + 16 * (base + 1))
                next_set(entries, (DOWN,))

            def last(b, u, j, base):
                h_lo(b + NT, u % 2)
                add_routed(b + NT, b, u, j * 16 + 16 * (base + 1))

            dve.wait_ge(tables, 1)
            next_set(table_entries(dve, 0, range(OTHER_COL, FLAG_COL + 3)), (DOWN,))
            groups(dve, step, last)

        @block.tensor
        def _(pe):
            pe.wait_ge(consts, N_CONSTS)
            for b in range(B):
                if b >= 2:
                    pe.wait_ge(bank_measured, 2 * (b - 1))
                    pe.wait_ge(squares, 2 * (b - 1))
                aT = GU[:, 2 * (b % 2):2 * (b % 2) + 2, :].rearrange("p a (h t) -> p (a h) t", t=TPB)
                for h in range(2):
                    t = 2 * b + h
                    pe.wait_ge(a_ready, t + 1)
                    for k in range(KC):
                        last = pe.transpose(aT[:, k, h * P:(h + 1) * P], tiles[:, t % RING, k * P:(k + 1) * P], ident[:, :])
                last.then_inc(aT_ready, 1)
            spread_in = scratch[:, 0:NV].rearrange("p (s r) -> p s r", s=KC * 3)
            pe.wait_ge(spread_ready, 1)
            pe.wait_ge(bank_measured, 2 * B)
            V = GU[:, 0:3, :].rearrange("p a c -> p (a c)")
            for s in range(KC * 3):
                last = pe.transpose(V[:, s * P:(s + 1) * P], spread_in[:, s, :], ident[:, :])
            last.then_inc(v_ready, 1)
            for i in range(SEARCH_STEPS):
                pe.wait_ge(below, i + 1)
                pe.matmul(yb[:, 0:1], same_batch[:, :, :].rearrange("p b r -> p (b r)"), search[:, 2:3], start=True, stop=True).then_inc(n_below, 1)
            pe.wait_ge(med_diag_ready, 1)
            pe.matmul(yb[:, 8:8 + B], ones[:, :], med_diag[:, :], start=True, stop=True).then_inc(medians_ready, 1)

            def spread_gate(b):
                if not (isinstance(b, int) and b == 0):
                    pe.wait_ge(gate_used, 2 * b if isinstance(b, int) else b * 2)
                for part in (HI, LO):
                    pe.wait_ge(diag_ready, b * 2 + (1 + part))
                    mm = pe.matmul(mb[:, :], ones_r[:, :], diag[:, part, :], start=(part == HI), stop=(part == LO))
                    mm.then_inc(gates_spread, 1)

            def transpose_x(n, src):
                if not (isinstance(n, int) and n == 0):
                    pe.wait_ge(xlo, n)
                for k in range(KC):
                    last = pe.transpose(tx[:, k * P:(k + 1) * P], src[:, k * P:(k + 1) * P], ident[:, :])
                last.then_inc(tx_done, 1)

            def transpose_h(n, parity):
                pe.wait_ge(hid_ready, n + 1)
                for k in range(KC):
                    last = pe.transpose(th[:, k * P:(k + 1) * P], hidden[:, parity, k * P:(k + 1) * P], ident[:, :])
                last.then_inc(th_done, 1)

            def product(dst, left, q, k):
                i = 0
                for kc in range(KC):
                    for lp, wp in ((HI, HI), (HI, LO), (LO, HI)):
                        last = pe.matmul(dst, left[:, lp, kc, :], wset(q, k, wp, kc), start=(i == 0), stop=(i == 3 * KC - 1))
                        i += 1
                return last

            def gate_product(n, slot, parity, q, before):
                pe.wait_ge(wlo, before + 1)
                pe.wait_ge(xlo, n + 1)
                product(gu(parity, GATE), xT[:, slot], q, GATE).then_inc(g_done, 1)

            def up_product(n, slot, parity, q, before):
                pe.wait_ge(wlo, before + 2)
                product(gu(parity, UP), xT[:, slot], q, UP).then_inc(u_done, 1)

            def down_product(n, parity, q, before):
                pe.wait_ge(wlo, before + 3)
                pe.wait_ge(hlo, n + 1)
                product(yb[:, :], hT[:, parity], q, DOWN).then_inc(y_done, 1)

            def route(t, slot):
                pe.wait_ge(xlo, t + 1)
                if not (isinstance(t, int) and t == 0):
                    pe.wait_ge(logits_used, t)
                for kc in range(KC):
                    for lp in (HI, LO):
                        last = pe.matmul(th[:, 0:2 * E], xT[:, slot, lp, kc, :], router_parts[:, kc, :, :].rearrange("p h e -> p (h e)"),
                                         start=(kc == 0 and lp == HI), stop=(kc == KC - 1 and lp == LO))
                last.then_inc(logits, 1)

            def prepare(t):
                pe.wait_ge(xn_ready, t + 1)
                transpose_x(t, tiles[:, t, :])

            pe.wait_ge(router_ready, 1)
            spread_gate(0)
            spread_gate(1)
            prepare(0)
            prepare(1)
            gate_product(0, 0, 0, 0, 0)
            prepare(2)
            route(0, 0)
            route(1, 1)
            prepare(3)
            up_product(0, 0, 0, 0, 0)
            route(2, 2)
            spread_gate(2)
            route(3, 3)
            with pe.Fori(0, NT // RING - 1) as j:
                for u in range(RING):
                    n = j * RING + u
                    gate_product(n + 1, (u + 1) % RING, (u + 1) % 2, 0, 0)
                    pe.wait_ge(logits_used, n + RING)
                    transpose_h(n, u % 2)
                    up_product(n + 1, (u + 1) % RING, (u + 1) % 2, 0, 0)
                    pe.wait_ge(xn_ready, n + RING + 1)
                    transpose_x(n + RING, tiles[:, u, :])
                    if u % 2 == 1:
                        spread_gate(j * 2 + (3 + u // 2))
                    down_product(n, u % 2, 0, 0)
                    route(n + RING, u)

            def rank():
                pe.wait_ge(chosen_ready, 1)
                oh = chosen_flat()
                pe.matmul(mb[:, RANKS], upper[:, :], oh, start=True, stop=False)
                for i in range(NT - 1):
                    pe.matmul(mb[:, (i + 1) * E:NT * E].rearrange("p (t e) -> p t e", e=E), ones_bf[:, :],
                              oh[:, i * E:(i + 1) * E].unsqueeze(1).to_broadcast([P, NT - 1 - i, E]),
                              start=False, stop=(i == NT - 2))
                for i in range(NT):
                    last = pe.matmul(mb[:, COUNTS], ones_bf[:, :], oh[:, i * E:(i + 1) * E], start=(i == 0), stop=(i == NT - 1))
                last.then_inc(rank_done, 1)

            def fill_slots():
                inblk, sel = slot_matrices()
                pe.wait_ge(sel_ready, 1 + FIELDS)
                for i in range(NT):
                    last = pe.matmul(mb[:, SLOTS], inblk[:, i, :], sel[:, i, :], start=(i == 0), stop=(i == NT - 1))
                last.then_inc(slots_done, 1)

            n = NT - RING
            gate_product(n + 1, 1, 1, 0, 0)
            pe.wait_ge(logits_used, NT)
            transpose_h(n, 0)
            up_product(n + 1, 1, 1, 0, 0)
            rank()
            down_product(n, 0, 0, 0)
            gate_product(n + 2, 2, 0, 0, 0)
            transpose_h(n + 1, 1)
            up_product(n + 2, 2, 0, 0, 0)
            down_product(n + 1, 1, 0, 0)
            gate_product(n + 3, 3, 1, 0, 0)
            fill_slots()
            transpose_h(n + 2, 0)
            up_product(n + 3, 3, 1, 0, 0)
            down_product(n + 2, 0, 0, 0)
            pe.wait_ge(xg_in[0], 16)
            transpose_x(n + 4, xg[:, 0, :])
            transpose_h(n + 3, 1)
            gate_product(n + 4, 0, 0, 1, 3)
            down_product(n + 3, 1, 0, 0)
            pe.wait_ge(xg_in[1], 16)
            transpose_x(n + 5, xg[:, 1, :])
            up_product(n + 4, 0, 0, 1, 3)

            def step(b, u, j, base):
                n = b + NT
                ahead = (u + 2) % RING
                q, ready, q_after, ready_after = table_entries(pe, b, range(SLOT_COL, READY2_COL + 1))
                gate_product(n + 1, 1 - u % 2, 1 - u % 2, q_after, ready_after)
                transpose_h(n, u % 2)
                up_product(n + 1, 1 - u % 2, 1 - u % 2, q_after, ready_after)
                pe.wait_ge(xg_in[ahead], j * 16 + 16 * (base + 1 + (u + 2) // RING))
                transpose_x(n + 2, xg[:, ahead, :])
                down_product(n, u % 2, q, ready)

            def last(b, u, j, base):
                q, ready = table_entries(pe, b, range(SLOT_COL, READY_COL + 1))
                transpose_h(b + NT, u % 2)
                down_product(b + NT, u % 2, q, ready)

            pe.wait_ge(tables, 1)
            groups(pe, step, last)


def kernel(x, L0_conv_cfc_w, L0_conv_bn_w, L0_conv_bn_b, L0_ffn_router_w, L0_ffn_w1, L0_ffn_v1, L0_ffn_w2,
           L0_ffn_shared_gate, L0_ffn_shared_up, L0_ffn_shared_down):
    import numpy as np
    import concourse.bacc as bacc
    from concourse.bass_utils import run_bass_kernel_spmd

    x = np.asarray(x)
    batch, chans, height, width = x.shape
    kc = chans // P

    def chunks(a):
        a = np.asarray(a).reshape(kc, P, -1)
        return np.ascontiguousarray(a.transpose(1, 0, 2)).reshape(P, -1)

    x_tok = np.ascontiguousarray(x.transpose(0, 2, 3, 1)).reshape(-1, chans)
    cfc = np.asarray(L0_conv_cfc_w)[:, [0, 2, 1]]
    conv_par = np.concatenate([chunks(cfc), chunks(L0_conv_bn_w), chunks(L0_conv_bn_b)], axis=1)
    router = chunks(np.asarray(L0_ffn_router_w).T)
    shared = [np.asarray(a).T for a in (L0_ffn_shared_gate, L0_ffn_shared_up, L0_ffn_shared_down)]
    sets = [shared] + [[np.asarray(a)[e] for a in (L0_ffn_w1, L0_ffn_v1, L0_ffn_w2)] for e in range(len(L0_ffn_w1))]
    weights = np.stack([np.stack([chunks(m) for m in one]) for one in sets])

    nc = bacc.Bacc("TRN2", target_bir_lowering=False, num_devices=1)
    arrays = {"x_tok": x_tok, "conv_par": conv_par, "router": router, "weights": weights}
    ins = [nc.dram_tensor(n, a.shape, F32, kind="ExternalInput").ap() for n, a in arrays.items()]
    xn_d = nc.dram_tensor("xn_d", x_tok.shape, F32).ap()
    z_d = nc.dram_tensor("z_d", x_tok.shape, F32).ap()
    out = nc.dram_tensor("out", x_tok.shape, F32, kind="ExternalOutput").ap()
    program(nc, batch, *ins, xn_d, z_d, out)
    r = run_bass_kernel_spmd(nc, [arrays], core_ids=[0])
    got = r.results[0]["out"]
    return np.ascontiguousarray(got.reshape(batch, height, width, chans).transpose(0, 3, 1, 2))
```
